# Optimizing a Trainium2 kernel written in Bass

```python
import numpy as np
import jax
import jax.numpy as jnp

def _softmax(x, axis=-1):
    return jax.nn.softmax(x, axis=axis)

def _gelu(x):
    return jax.nn.gelu(x, approximate=True)

def _silu(x):
    return jax.nn.silu(x)

def _sigmoid(x):
    return jax.nn.sigmoid(x)

def _layernorm(x, axis=-1, eps=1e-05):
    m = jnp.mean(x, axis=axis, keepdims=True)
    v = jnp.var(x, axis=axis, keepdims=True)
    return (x - m) / jnp.sqrt(v + eps)

def _scatter_add(tgt, idx, src, axis=0):
    return tgt.at[idx].add(src)

def _segment_sum(src, seg, n):
    return jax.ops.segment_sum(src, seg, n)
kernel_name = 'mk_vit_tower_d1_tok_img256_r4_f80869'

def setup_inputs(seed: int=0):
    np.random.seed(seed)
    _w = jnp.asarray

    def _rec_inputs():
        import jax
        import jax.numpy as jnp
        _rk = jax.random.key(seed)
        x = 7.22013e-05 + 1.00017 * jax.random.normal(jax.random.fold_in(_rk, 1), (16, 1, 224, 224), jnp.float32)
        return x
    x = _rec_inputs()

    def _L0_tok_setup():
        import jax, jax.numpy as jnp
        import numpy as np
        P = 8
        C = 1
        D = 64
        key = jax.random.key(seed)
        k1, k2, k3 = jax.random.split(key, 3)
        x = jax.random.normal(k1, (128, C, 64, 64), dtype=jnp.float32)
        patch_dim = P * P * C
        bound = 1.0 / np.sqrt(patch_dim)
        W = jax.random.uniform(k2, (D, patch_dim), dtype=jnp.float32, minval=-bound, maxval=bound)
        b = jax.random.uniform(k3, (D,), dtype=jnp.float32, minval=-bound, maxval=bound)
        return {'x': x, 'W': W, 'b': b}
    _L0_tok_all = _L0_tok_setup()
    _L0_tok_in = {k: v for k, v in _L0_tok_all.items() if k in ('W', 'b')}
    del _L0_tok_all

    def _L0_attn_setup():
        import jax, jax.numpy as jnp
        import numpy as np
        SEQ, BATCH, IN, HID = (512, 64, 64, 64)
        key = jax.random.key(seed)
        k1, k2, k3, k4, k5 = jax.random.split(key, 5)
        s = 1.0 / np.sqrt(HID)
        return {'x_in': jax.random.normal(k1, (SEQ, BATCH, IN), dtype=jnp.float32), 'W_ih': jax.random.uniform(k2, (HID, IN), jnp.float32, -s, s), 'W_hh': jax.random.uniform(k3, (HID, HID), jnp.float32, -s, s), 'b_ih': jax.random.uniform(k4, (HID,), jnp.float32, -s, s), 'b_hh': jax.random.uniform(k5, (HID,), jnp.float32, -s, s)}
    _L0_attn_all = _L0_attn_setup()
    _L0_attn_in = {k: v for k, v in _L0_attn_all.items() if k in ('W_ih', 'W_hh', 'b_ih', 'b_hh')}
    del _L0_attn_all

    def _L0_ffn_setup():
        import jax, jax.numpy as jnp
        import numpy as np
        B, S, H, F, E, K = (8, 1024, 64, 128, 16, 2)
        EPS = 1e-05
        key = jax.random.key(seed)
        ks = jax.random.split(key, 9)
        sc = 0.02
        return {'x': jax.random.normal(ks[0], (B, S, H), dtype=jnp.float32), 'gate_w': jax.random.normal(ks[1], (H, E), dtype=jnp.float32) * sc, 'gate_b': jnp.zeros((E,), dtype=jnp.float32), 'w1': jax.random.normal(ks[2], (E, H, F), dtype=jnp.float32) * sc, 'b1': jnp.zeros((E, F), dtype=jnp.float32), 'w2': jax.random.normal(ks[3], (E, F, H), dtype=jnp.float32) * sc, 'b2': jnp.zeros((E, H), dtype=jnp.float32), 'gamma': jnp.ones((H,), dtype=jnp.float32), 'beta': jnp.zeros((H,), dtype=jnp.float32)}
    _L0_ffn_all = _L0_ffn_setup()
    _L0_ffn_in = {k: v for k, v in _L0_ffn_all.items() if k in ('gate_w', 'gate_b', 'w1', 'b1', 'w2', 'b2', 'gamma', 'beta')}
    del _L0_ffn_all
    return {'x': x, 'L0_tok_W': _L0_tok_in['W'], 'L0_tok_b': _L0_tok_in['b'], 'L0_attn_W_ih': _L0_attn_in['W_ih'], 'L0_attn_W_hh': _L0_attn_in['W_hh'], 'L0_attn_b_ih': _L0_attn_in['b_ih'], 'L0_attn_b_hh': _L0_attn_in['b_hh'], 'L0_ffn_gate_w': _L0_ffn_in['gate_w'], 'L0_ffn_gate_b': _L0_ffn_in['gate_b'], 'L0_ffn_w1': _L0_ffn_in['w1'], 'L0_ffn_b1': _L0_ffn_in['b1'], 'L0_ffn_w2': _L0_ffn_in['w2'], 'L0_ffn_b2': _L0_ffn_in['b2'], 'L0_ffn_gamma': _L0_ffn_in['gamma'], 'L0_ffn_beta': _L0_ffn_in['beta']}

def reference(x, L0_tok_W, L0_tok_b, L0_attn_W_ih, L0_attn_W_hh, L0_attn_b_ih, L0_attn_b_hh, L0_ffn_gate_w, L0_ffn_gate_b, L0_ffn_w1, L0_ffn_b1, L0_ffn_w2, L0_ffn_b2, L0_ffn_gamma, L0_ffn_beta):
    import jax
    import jax.numpy as jnp

    def _L0_tok_ref(x, W, b):
        import jax, jax.numpy as jnp
        import numpy as np
        P = 8
        C = 1
        D = 64
        B, c, h, w = x.shape
        p = P
        xp = x.reshape(B, c, h // p, p, w // p, p)
        xp = jnp.transpose(xp, (0, 2, 4, 3, 5, 1))
        xp = xp.reshape(B, h // p * (w // p), p * p * c)
        return jnp.einsum('bnk,dk->bnd', xp, W) + b

    def _L0_attn_ref(x_in, W_ih, W_hh, b_ih, b_hh):
        import jax, jax.numpy as jnp
        import numpy as np
        SEQ, BATCH, IN, HID = (512, 64, 64, 64)
        xp = jnp.einsum('tbi,hi->tbh', x_in, W_ih) + b_ih + b_hh
        h0 = jnp.zeros((x_in.shape[1], W_hh.shape[0]), dtype=x_in.dtype)

        def step(h, xp_t):
            h_new = jnp.tanh(xp_t + h @ W_hh.T)
            return (h_new, h_new)
        _, hiddens = jax.lax.scan(step, h0, xp)
        return hiddens

    def _L0_ffn_ref(x, gate_w, gate_b, w1, b1, w2, b2, gamma, beta):
        import jax, jax.numpy as jnp
        import numpy as np
        B, S, H, F, E, K = (8, 1024, 64, 128, 16, 2)
        EPS = 1e-05
        gate_logits = x @ gate_w + gate_b
        topk_vals, topk_idx = jax.lax.top_k(gate_logits, K)
        topk_w = jax.nn.softmax(topk_vals, axis=-1)
        h = jax.nn.relu(jnp.einsum('bsh,ehf->bsef', x, w1) + b1)
        expert_out = jnp.einsum('bsef,efh->bseh', h, w2) + b2
        sel = jnp.take_along_axis(expert_out, topk_idx[:, :, :, None], axis=2)
        moe = jnp.sum(topk_w[..., None] * sel, axis=2)
        y = x + moe
        mu = jnp.mean(y, axis=-1, keepdims=True)
        var = jnp.var(y, axis=-1, keepdims=True)
        return (y - mu) / jnp.sqrt(var + EPS) * gamma + beta
    h = _L0_tok_ref(x, L0_tok_W, L0_tok_b)
    h = h + _L0_attn_ref(_layernorm(h, axis=-1), L0_attn_W_ih, L0_attn_W_hh, L0_attn_b_ih, L0_attn_b_hh)
    h = h + _L0_ffn_ref(_layernorm(h, axis=-1), L0_ffn_gate_w, L0_ffn_gate_b, L0_ffn_w1, L0_ffn_b1, L0_ffn_w2, L0_ffn_b2, L0_ffn_gamma, L0_ffn_beta)
    return h

_drawn_inputs = setup_inputs


def setup_inputs(seed=0):
    import zlib

    import numpy as np

    out = dict(_drawn_inputs(seed))
    spreads = {'L0_ffn_gate_b': (0.0, 0.1),
     'L0_ffn_b1': (0.0, 0.8),
     'L0_ffn_b2': (0.0, 0.1),
     'L0_ffn_gamma': (1.0, 0.2),
     'L0_ffn_beta': (0.0, 0.1)}
    factors = {'L0_ffn_w1': 6.298, 'L0_ffn_w2': 4.721}
    for name, (base, spread) in spreads.items():
        noise = np.random.default_rng([zlib.crc32(name.encode()), seed]).standard_normal(out[name].shape)
        drawn = base * np.exp(spread * noise) if base else spread * noise
        out[name] = jnp.asarray(drawn.astype(out[name].dtype))
    for name, factor in factors.items():
        out[name] = (out[name] * factor).astype(out[name].dtype)
    return out
```

```python
import concourse.bass as bass
from concourse import mybir
from contextlib import ExitStack


def vit_tower_kernel(nc, x_in, tok_w, tok_b, w_ih, w_hh, b_ih, b_hh, gate_w, gate_b,
                     w1, b1, w2, b2, gamma, beta, out):
    f32 = mybir.dt.float32
    f32r = mybir.dt.float32r
    i32 = mybir.dt.int32
    ALU = mybir.AluOpType
    ACT = mybir.ActivationFunctionType
    X = mybir.AxisListType.X

    D = w_ih.shape[0]
    STEPS = out.shape[0]
    P = out.shape[1]
    TILES = out.shape[2]
    TOK = P * TILES
    E = w1.shape[1]
    F = w1.shape[2]
    K_IN = tok_w.shape[0]
    PAIRS = (TILES + 1) // 2
    EVEN = 2 * PAIRS
    HALF = P * PAIRS
    REST = TOK - HALF
    EPS = 1e-5
    FAR = -1.0e30
    PROD = 4
    assert 2 * D == 128 and F == 128 and HALF <= 512 and EVEN * D <= 512 and TILES * E == P

    ctx = ExitStack()
    with ctx:
        def sb(name, shape, dt=f32):
            return ctx.enter_context(nc.sbuf_tensor(name, shape, dt))

        def sem(name):
            return ctx.enter_context(nc.semaphore(name))

        tokw = sb("tokw", [K_IN + 1, D])
        wih = sb("wih", [2 * D, 2 * D])
        whh = sb("whh", [2 * D, 2 * D])
        rbias = sb("rbias", [2 * D, 2])
        rb = sb("rb", [2 * D, 1])
        w1f = sb("w1f", [2 * D, E, F])
        w1hi = sb("w1hi", [2 * D, E, F], f32r)
        w1lo = sb("w1lo", [2 * D, E, F], f32r)
        gwf = sb("gwf", [2 * D, E])
        gwhi = sb("gwhi", [2 * D, E], f32r)
        gwlo = sb("gwlo", [2 * D, E], f32r)
        b1c = sb("b1c", [F, E])
        w2s = sb("w2s", [F, E, D])
        b2d = sb("b2d", [P, TILES, D])
        gbias = sb("gbias", [P, E])
        gam = sb("gam", [P, D])
        bet = sb("bet", [P, D])
        ident = sb("ident", [128, 128])
        rank_i = sb("rank_i", [P, E], i32)
        rank = sb("rank", [P, E])
        nhalf = sb("nhalf", [P, TILES])

        xcur = sb("xcur", [K_IN + 1, TOK])
        h1 = sb("h1", [P, TILES, D])
        cen1 = sb("cen1", [P, TILES, D])
        sq1 = sb("sq1", [P, TILES, D])
        st1 = sb("st1", [P, 4, TILES])
        xn1 = sb("xn1", [P, EVEN, D])
        xn1t = sb("xn1t", [2 * D, HALF])
        hid = sb("hid", [2 * D, HALF])
        h2 = [sb(f"h2_{i}", [P, TILES, D]) for i in range(2)]
        h2b = sb("h2b", [P, TILES, D])
        cen2 = sb("cen2", [P, TILES, D])
        sq2 = sb("sq2", [P, TILES, D])
        st2 = sb("st2", [P, 4, TILES])
        x2 = sb("x2", [P, TILES, D])
        x2hi = sb("x2hi", [P, TILES, D], f32r)
        x2hl = sb("x2hl", [P, TILES, 2, D])
        xt = [sb(f"xt{i}", [2 * D, TOK], f32r) for i in range(2)]
        lg = sb("lg", [P, TILES, E])
        hit = sb("hit", [P, TILES, E])
        best = [sb(f"best{i}", [P, TILES, E]) for i in range(2)]
        tv = sb("tv", [P, 10, TILES])
        gates = [sb(f"gates{i}", [P, TILES, E]) for i in range(2)]
        gt = sb("gt", [P, P])
        hexp = [sb(f"hexp{i}", [F, TOK]) for i in range(2)]
        prod = [sb(f"prod{i}", [P, TILES, D]) for i in range(PROD)]
        acc = [sb(f"acc{i}", [P, TILES, D]) for i in range(2)]
        cen3 = sb("cen3", [P, TILES, D])
        sq3 = sb("sq3", [P, TILES, D])
        st3 = sb("st3", [P, 4, TILES])
        yn = sb("yn", [P, TILES, D])
        yo = sb("yo", [P, TILES, D])

        bank = [ctx.enter_context(nc.psum_tensor(f"bank{i}", [128, 1024], f32)) for i in range(2)]
        pY = [ctx.enter_context(nc.psum_tensor(f"pY{i}", [128, 512], f32)) for i in range(2)]
        pA = ctx.enter_context(nc.psum_tensor("pA", [128, 512], f32))
        pB = ctx.enter_context(nc.psum_tensor("pB", [128, 512], f32))

        class Chain:

            def __init__(self, name, stages):
                self.sem, self.stages = sem(name), stages

            def at(self, step, stage):
                return step * len(self.stages) + self.stages.index(stage) + 1

            def wait(self, eng, step, stage):
                eng.wait_ge(self.sem, self.at(step, stage))

        EMBED = Chain("embed_stage", ["h1", "sum", "center", "square", "sumsq", "var", "rstd", "norm",
                                      "turned", "xn1t"])
        MIX = Chain("mix_stage", ["pre", "hid", "hid_turned", "h2", "sum", "center", "square", "sumsq", "var",
                                  "rstd", "x2", "hi", "copy_hi", "lo", "turned_a", "turned_b", "xt_a", "xt_b",
                                  "logits", "biased", "max1", "hit1", "ranked1", "first1", "best1",
                                  "without", "max2", "hit2", "ranked2", "first2", "best2",
                                  "diff", "exp", "den", "p1", "p2", "g1", "g2", "gates",
                                  "gates_turned", "gt", "bias2", "acc"])
        CLOSE = Chain("close_stage", ["sum", "center", "square", "sumsq", "var", "rstd", "norm", "gamma", "out"])

        wload = sem("weights_loaded")
        xload = sem("x_loaded")
        consts = sem("constants_set")
        dve_consts = sem("vector_constants_set")
        h1_kept = sem("h1_kept")
        h2b_set = sem("h2b_set")
        z_ready = sem("z_ready")
        h_ready = sem("h_ready")
        y_ready = sem("y_ready")
        p_ready = sem("product_ready")
        summed = sem("product_summed")
        stored = sem("out_stored")

        def z_of(n):
            return bank[n % 2][:, :].rearrange("p (b c) -> p b c", b=2)

        def tiles_of(ps, n=TILES):
            return ps[0:P, 0:n * D].rearrange("p (i d) -> p i d", d=D)

        def over_d(ap):
            return ap.unsqueeze(2).to_broadcast([P, TILES, D])

        def over_e(ap):
            return ap.unsqueeze(2).to_broadcast([P, TILES, E])

        def over_tiles(ap, n):
            return ap.unsqueeze(1).to_broadcast([P, TILES, n])

        def run(eng, body):
            body(-1, 1, experts=False, embed=True, mix=True, close=False)
            body(0, 0, experts=True, embed=True, mix=True, close=False)
            with eng.Fori(1, STEPS - 3, 2) as t:
                body(t, 1, experts=True, embed=True, mix=True, close=True)
                body(t + 1, 0, experts=True, embed=True, mix=True, close=True)
            body(STEPS - 3, 1, experts=True, embed=True, mix=True, close=True)
            body(STEPS - 2, 0, experts=True, embed=False, mix=True, close=True)
            body(STEPS - 1, 1, experts=True, embed=False, mix=False, close=True)
        assert (STEPS - 4) % 2 == 0

        block = ctx.enter_context(nc.Block())

        NW = 0
        FILLS = 8

        @block.sync
        def _(sp):
            nonlocal NW
            sp.dma_start(xcur[0:K_IN, :], x_in[:, 0:TOK]).then_inc(xload, 16)
            loads = [(tokw[0:K_IN, :], tok_w), (tokw[K_IN:K_IN + 1, :], tok_b.unsqueeze(0))]
            for k in range(2):
                half = slice(k * D, (k + 1) * D)
                loads += [(wih[half, half], w_ih), (whh[half, half], w_hh),
                          (rbias[half, 0:1], b_ih.unsqueeze(1)), (rbias[half, 1:2], b_hh.unsqueeze(1)),
                          (gwf[half, :], gate_w), (w1f[half, :, :], w1)]
            loads += [(b1c[:, :], b1), (w2s[:, :, :], w2),
                      (gbias[:, :], gate_b.partition_broadcast(P)), (gam[:, :], gamma.partition_broadcast(P)),
                      (bet[:, :], beta.partition_broadcast(P))]
            loads += [(b2d[i * E:(i + 1) * E, i, :], b2) for i in range(TILES)]
            sp.wait_ge(consts, FILLS)
            for dst, src in loads:
                sp.dma_start(dst, src).then_inc(wload, 16)
            NW = 16 * len(loads)

            def load(s):
                EMBED.wait(sp, s - 1, "h1")
                sp.dma_start(xcur[0:K_IN, :], x_in[:, bass.ds(s * TOK, TOK)]).then_inc(xload, 16)

            def store(s):
                CLOSE.wait(sp, s, "out")
                sp.dma_start(out[bass.ds(s, 1), :, :, :].rearrange("s p i d -> (s p) i d"),
                             yo[:, :, :]).then_inc(stored, 16)

            load(1)
            load(2)
            with sp.Fori(3, STEPS) as s:
                load(s)
                store(s - 3)
            with sp.Fori(STEPS - 3, STEPS) as s:
                store(s)
            sp.wait_ge(stored, 16 * STEPS)

        @block.gpsimd
        def _(pool):
            zeros = [wih[:, :], whh[:, :], b2d[:, :, :], xn1[:, :, :], hid[:, :], ident[:, :]]
            fills = [(z, 0.0) for z in zeros] + [(nhalf[:, :], -0.5), (xcur[K_IN:K_IN + 1, :], 1.0)]
            for k, (dst, value) in enumerate(fills):
                if k:
                    pool.wait_ge(consts, k)
                nc.gpsimd.memset(dst, value).then_inc(consts, 1)
            pool.wait_ge(consts, len(fills))
            nc.gpsimd.iota(rank_i[:, :], pattern=[[-1, E]], base=E, channel_multiplier=0).then_inc(consts, 1)
            pool.wait_ge(consts, FILLS + 1)
            nc.gpsimd.affine_select(out=ident[:, :], in_=ident[:, :], compare_op=ALU.not_equal, fill=1.0,
                                    base=0, pattern=[[-1, 128]], channel_multiplier=1).then_inc(consts, 1)
            pool.wait_ge(wload, NW)

            def body(t, par, experts, embed, mix, close):
                def add(n_step, e, p):
                    n = n_step * E + e
                    pool.wait_ge(p_ready, n + 1)
                    if e == 0:
                        MIX.wait(pool, n_step, "acc")
                    else:
                        pool.wait_ge(summed, n)
                    nc.gpsimd.tensor_tensor(acc[p][:, :, :], acc[p][:, :, :], prod[e % PROD][:, :, :],
                                            ALU.add).then_inc(summed, 1)

                for u in range(E):
                    if experts:
                        if u >= 1:
                            add(t, u - 1, par)
                        elif isinstance(t, int) and t == 0:
                            pass
                        else:
                            add(t - 1, E - 1, 1 - par)
                    if mix and u == 5:
                        MIX.wait(pool, t + 1, "var")
                        nc.gpsimd.tensor_tensor(st2[:, 3, :], st2[:, 2, :], nhalf[:, :], ALU.pow)\
                            .then_inc(MIX.sem, 1)
                    if close and u == 8:
                        CLOSE.wait(pool, t - 1, "var")
                        nc.gpsimd.tensor_tensor(st3[:, 3, :], st3[:, 2, :], nhalf[:, :], ALU.pow)\
                            .then_inc(CLOSE.sem, 1)
                    if embed and u == 9:
                        EMBED.wait(pool, t + 2, "var")
                        nc.gpsimd.tensor_tensor(st1[:, 3, :], st1[:, 2, :], nhalf[:, :], ALU.pow)\
                            .then_inc(EMBED.sem, 1)
                if experts:
                    if close:
                        CLOSE.wait(pool, t - 1, "out")
                    MIX.wait(pool, t, "h2")
                    nc.gpsimd.tensor_tensor(h2b[:, :, :], h2[par][:, :, :], over_tiles(bet[:, :], D), ALU.add)\
                        .then_inc(h2b_set, 1)

            EMBED.wait(pool, 0, "var")
            nc.gpsimd.tensor_tensor(st1[:, 3, :], st1[:, 2, :], nhalf[:, :], ALU.pow).then_inc(EMBED.sem, 1)
            run(pool, body)
            pool.wait_ge(p_ready, STEPS * E)
            pool.wait_ge(summed, STEPS * E - 1)
            p = (STEPS - 1) % 2
            nc.gpsimd.tensor_tensor(acc[p][:, :, :], acc[p][:, :, :], prod[(E - 1) % PROD][:, :, :],
                                    ALU.add).then_inc(summed, 1)
            CLOSE.wait(pool, STEPS - 1, "var")
            nc.gpsimd.tensor_tensor(st3[:, 3, :], st3[:, 2, :], nhalf[:, :], ALU.pow).then_inc(CLOSE.sem, 1)

        @block.scalar
        def _(act):
            act.wait_ge(wload, NW)
            nc.scalar.activation(w1hi[:, :, :], w1f[:, :, :], ACT.Copy).then_inc(dve_consts, 1)
            nc.scalar.activation(gwhi[:, :], gwf[:, :], ACT.Copy).then_inc(dve_consts, 1)
            act.wait_ge(dve_consts, 4)

            def keep_h1(s):
                EMBED.wait(act, s, "h1")
                if not (isinstance(s, int) and s == 0):
                    MIX.wait(act, s - 1, "h2")
                nc.scalar.activation(h1[:, :, :], tiles_of(pA), ACT.Copy).then_inc(h1_kept, 1)

            def square(chain, s, dst, src):
                chain.wait(act, s, "center")
                nc.scalar.activation(dst[:, :, :], src[:, :, :], ACT.Square).then_inc(chain.sem, 1)

            def keep_xn1t(s):
                EMBED.wait(act, s, "turned")
                if not (isinstance(s, int) and s == 0):
                    MIX.wait(act, s - 1, "pre")
                nc.scalar.activation(xn1t[:, :], pA[:, 0:HALF], ACT.Copy).then_inc(EMBED.sem, 1)

            def body(t, par, experts, embed, mix, close):
                new = 1 - par
                for u in range(E):
                    if experts:
                        n = t * E + u
                        act.wait_ge(z_ready, n + 1)
                        if not isinstance(n, int) or n >= 2:
                            act.wait_ge(y_ready, n - 1)
                        nc.scalar.activation(hexp[u % 2][:, 0:HALF], z_of(u)[:, 0, 0:HALF], ACT.Relu,
                                             bias=b1c[:, u:u + 1])
                        nc.scalar.activation(hexp[u % 2][:, HALF:TOK], z_of(u)[:, 1, 0:REST], ACT.Relu,
                                             bias=b1c[:, u:u + 1]).then_inc(h_ready, 1)
                    if mix and u == 0:
                        MIX.wait(act, t + 1, "pre")
                        nc.scalar.activation(hid[:, :], pA[:, 0:HALF], ACT.Tanh, bias=rb[:, 0:1])\
                            .then_inc(MIX.sem, 1)
                    if mix and u == 4:
                        square(MIX, t + 1, sq2, cen2)
                    if embed and u == 4:
                        keep_h1(t + 2)
                    if mix and u == 6:
                        MIX.wait(act, t + 1, "x2")
                        nc.scalar.activation(x2hi[:, :, :], x2[:, :, :], ACT.Copy).then_inc(MIX.sem, 1)
                        MIX.wait(act, t + 1, "hi")
                        nc.scalar.activation(x2hl[:, :, 0, :], x2hi[:, :, :].bitcast(f32), ACT.Copy)\
                            .then_inc(MIX.sem, 1)
                    if close and u == 6:
                        square(CLOSE, t - 1, sq3, cen3)
                    if embed and u == 8:
                        square(EMBED, t + 2, sq1, cen1)
                    if mix and u == 8:
                        MIX.wait(act, t + 1, "turned_b")
                        nc.scalar.activation(xt[new][:, 0:HALF], pB[:, 0:HALF], ACT.Copy).then_inc(MIX.sem, 1)
                    if embed and u == 12:
                        keep_xn1t(t + 2)
                    if mix and u == 12:
                        MIX.wait(act, t + 1, "diff")
                        nc.scalar.activation(tv[:, 5, :], tv[:, 4, :], ACT.Exp).then_inc(MIX.sem, 1)
                    if mix and u == 14:
                        MIX.wait(act, t + 1, "gates_turned")
                        nc.scalar.activation(gt[:, :], pB[0:P, 0:P], ACT.Copy).then_inc(MIX.sem, 1)

            keep_h1(0)
            square(EMBED, 0, sq1, cen1)
            keep_xn1t(0)
            run(act, body)
            square(CLOSE, STEPS - 1, sq3, cen3)

        @block.vector
        def _(dve):
            dve.wait_ge(wload, NW)
            dve.wait_ge(dve_consts, 2)
            nc.vector.tensor_tensor(w1lo[:, :, :], w1f[:, :, :], w1hi[:, :, :].bitcast(f32), ALU.subtract)\
                .then_inc(dve_consts, 1)
            nc.vector.tensor_tensor(rb[:, :], rbias[:, 0:1], rbias[:, 1:2], ALU.add).then_inc(dve_consts, 1)
            nc.vector.tensor_tensor(gwlo[:, :], gwf[:, :], gwhi[:, :].bitcast(f32), ALU.subtract)\
                .then_inc(dve_consts, 1)
            dve.wait_ge(consts, FILLS + 2)
            nc.vector.tensor_copy(rank[:, :], rank_i[:, :]).then_inc(dve_consts, 1)
            dve.wait_ge(dve_consts, 6)

            def norm_sum(chain, s, src, st):
                nc.vector.tensor_reduce(st[:, 0, :], src, X, ALU.add).then_inc(chain.sem, 1)

            def norm_center(chain, s, src, st, cen):
                chain.wait(dve, s, "sum")
                nc.vector.scalar_tensor_tensor(out=cen[:, :, :], in0=over_d(st[:, 0, :]), scalar=-1.0 / D,
                                               in1=src, op0=ALU.mult, op1=ALU.add).then_inc(chain.sem, 1)

            def norm_var(chain, s, sq, st):
                chain.wait(dve, s, "square")
                nc.vector.tensor_reduce(st[:, 1, :], sq[:, :, :], X, ALU.add).then_inc(chain.sem, 1)
                chain.wait(dve, s, "sumsq")
                nc.vector.tensor_scalar(st[:, 2, :], st[:, 1, :], 1.0 / D, EPS, ALU.mult, ALU.add)\
                    .then_inc(chain.sem, 1)

            def norm_scale(chain, s, cen, st, dst):
                chain.wait(dve, s, "rstd")
                nc.vector.tensor_tensor(dst, cen[:, :, :], over_d(st[:, 3, :]), ALU.mult).then_inc(chain.sem, 1)

            def embed_center(s):
                dve.wait_ge(h1_kept, s + 1)
                norm_sum(EMBED, s, h1[:, :, :], st1)
                norm_center(EMBED, s, h1[:, :, :], st1, cen1)

            def embed_norm(s):
                norm_scale(EMBED, s, cen1, st1, xn1[:, 0:TILES, :])

            def gate_chain(s, new):
                MIX.wait(dve, s, "logits")
                nc.vector.tensor_tensor(lg[:, :, :], pB[0:P, 0:TILES * E].rearrange("p (i e) -> p i e", e=E),
                                        over_tiles(gbias[:, :], E), ALU.add).then_inc(MIX.sem, 1)
                MIX.wait(dve, s, "biased")
                for k in range(2):
                    top, mark, one = tv[:, k, :], tv[:, 2 + k, :], best[k]
                    nc.vector.tensor_reduce(top, lg[:, :, :], X, ALU.max).then_inc(MIX.sem, 1)
                    MIX.wait(dve, s, f"max{k + 1}")
                    nc.vector.tensor_tensor(hit[:, :, :], lg[:, :, :], over_e(top), ALU.is_equal).then_inc(MIX.sem, 1)
                    MIX.wait(dve, s, f"hit{k + 1}")
                    nc.vector.tensor_tensor(hit[:, :, :], hit[:, :, :], over_tiles(rank[:, :], E), ALU.mult)\
                        .then_inc(MIX.sem, 1)
                    MIX.wait(dve, s, f"ranked{k + 1}")
                    nc.vector.tensor_reduce(mark, hit[:, :, :], X, ALU.max).then_inc(MIX.sem, 1)
                    MIX.wait(dve, s, f"first{k + 1}")
                    nc.vector.tensor_tensor(one[:, :, :], hit[:, :, :], over_e(mark), ALU.is_equal).then_inc(MIX.sem, 1)
                    MIX.wait(dve, s, f"best{k + 1}")
                    if k == 0:
                        nc.vector.scalar_tensor_tensor(out=lg[:, :, :], in0=one[:, :, :], scalar=FAR,
                                                       in1=lg[:, :, :], op0=ALU.mult, op1=ALU.add)\
                            .then_inc(MIX.sem, 1)
                        MIX.wait(dve, s, "without")
                nc.vector.tensor_tensor(tv[:, 4, :], tv[:, 1, :], tv[:, 0, :], ALU.subtract).then_inc(MIX.sem, 1)

            def gate_weights(s, new):
                MIX.wait(dve, s, "exp")
                nc.vector.tensor_scalar(tv[:, 6, :], tv[:, 5, :], 1.0, None, ALU.add).then_inc(MIX.sem, 1)
                MIX.wait(dve, s, "den")
                nc.vector.reciprocal(tv[:, 7, :], tv[:, 6, :]).then_inc(MIX.sem, 1)
                MIX.wait(dve, s, "p1")
                nc.vector.tensor_tensor(tv[:, 8, :], tv[:, 5, :], tv[:, 7, :], ALU.mult).then_inc(MIX.sem, 1)
                MIX.wait(dve, s, "p2")
                nc.vector.tensor_tensor(best[0][:, :, :], best[0][:, :, :], over_e(tv[:, 7, :]), ALU.mult)\
                    .then_inc(MIX.sem, 1)
                nc.vector.tensor_tensor(best[1][:, :, :], best[1][:, :, :], over_e(tv[:, 8, :]), ALU.mult)\
                    .then_inc(MIX.sem, 1)
                MIX.wait(dve, s, "g2")
                nc.vector.tensor_tensor(gates[new][:, :, :], best[0][:, :, :], best[1][:, :, :], ALU.add)\
                    .then_inc(MIX.sem, 1)

            def gate(step, e, p):
                n = step * E + e
                dve.wait_ge(y_ready, n + 1)
                if e == 0:
                    MIX.wait(dve, step, "gates")
                if not isinstance(n, int) or n >= PROD:
                    dve.wait_ge(summed, n - PROD + 1)
                nc.vector.tensor_tensor(prod[e % PROD][:, :, :], tiles_of(pY[e % 2]), over_d(gates[p][:, :, e]),
                                        ALU.mult).then_inc(p_ready, 1)

            def close_center(s, p):
                dve.wait_ge(summed, s * E + E)
                norm_sum(CLOSE, s, acc[p][:, :, :], st3)
                norm_center(CLOSE, s, acc[p][:, :, :], st3, cen3)

            def close_out(s):
                norm_scale(CLOSE, s, cen3, st3, yn[:, :, :])
                CLOSE.wait(dve, s, "norm")
                nc.vector.tensor_tensor(yn[:, :, :], yn[:, :, :], over_tiles(gam[:, :], D), ALU.mult)\
                    .then_inc(CLOSE.sem, 1)
                CLOSE.wait(dve, s, "gamma")
                dve.wait_ge(h2b_set, s + 1)
                if not (isinstance(s, int) and s == 0):
                    dve.wait_ge(stored, 16 * s)
                nc.vector.tensor_tensor(yo[:, :, :], yn[:, :, :], h2b[:, :, :], ALU.add).then_inc(CLOSE.sem, 1)

            def body(t, par, experts, embed, mix, close):
                new = 1 - par
                s = t + 1
                for u in range(E):
                    if experts:
                        if u >= 1:
                            gate(t, u - 1, par)
                        elif not (isinstance(t, int) and t == 0):
                            gate(t - 1, E - 1, 1 - par)
                    if mix and u == 2:
                        MIX.wait(dve, s, "hid_turned")
                        dve.wait_ge(h1_kept, s + 1)
                        if not (isinstance(s, int) and s < 2):
                            dve.wait_ge(h2b_set, s - 1)
                        nc.vector.tensor_tensor(h2[new][:, :, :], tiles_of(pB), h1[:, :, :], ALU.add)\
                            .then_inc(MIX.sem, 1)
                        MIX.wait(dve, s, "h2")
                        norm_sum(MIX, s, h2[new][:, :, :], st2)
                    if mix and u == 3:
                        norm_center(MIX, s, h2[new][:, :, :], st2, cen2)
                    if close and u == 4:
                        close_center(t - 1, new)
                    if mix and u == 5:
                        norm_var(MIX, s, sq2, st2)
                    if mix and u == 6:
                        norm_scale(MIX, s, cen2, st2, x2[:, :, :])
                        MIX.wait(dve, s, "copy_hi")
                        nc.vector.tensor_tensor(x2hl[:, :, 1, :], x2[:, :, :], x2hi[:, :, :].bitcast(f32),
                                                ALU.subtract).then_inc(MIX.sem, 1)
                    if embed and u == 7:
                        embed_center(t + 2)
                    if close and u == 8:
                        norm_var(CLOSE, t - 1, sq3, st3)
                    if mix and u == 8:
                        MIX.wait(dve, s, "turned_b")
                        nc.vector.tensor_copy(xt[new][:, HALF:TOK], pA[:, 0:REST]).then_inc(MIX.sem, 1)
                    if embed and u == 9:
                        norm_var(EMBED, t + 2, sq1, st1)
                    if mix and u == 10:
                        gate_chain(s, new)
                    if embed and u == 11:
                        embed_norm(t + 2)
                    if mix and u == 12:
                        gate_weights(s, new)
                    if close and u == 13:
                        close_out(t - 1)
                    if mix and u == 15:
                        MIX.wait(dve, s, "bias2")
                        nc.vector.tensor_tensor(acc[new][:, :, :], tiles_of(pA), x2[:, :, :], ALU.add)\
                            .then_inc(MIX.sem, 1)

            embed_center(0)
            norm_var(EMBED, 0, sq1, st1)
            embed_norm(0)
            run(dve, body)
            last = STEPS - 1
            gate(last, E - 1, last % 2)
            close_center(last, last % 2)
            norm_var(CLOSE, last, sq3, st3)
            close_out(last)

        @block.tensor
        def _(pe):
            pe.wait_ge(wload, NW)
            pe.wait_ge(consts, FILLS + 2)
            pe.wait_ge(dve_consts, 6)

            def embed_in(s):
                pe.wait_ge(xload, 16 * s + 16)
                if not (isinstance(s, int) and s == 0):
                    MIX.wait(pe, s - 1, "hid")
                for i in range(TILES):
                    last = nc.tensor.matmul(tiles_of(pA)[:, i, :], xcur[:, i * P:(i + 1) * P], tokw[:, :],
                                            start=True, stop=True)
                last.then_inc(EMBED.sem, 1)

            def turn_pairs(dst, src, pairs, chain):
                for i in range(pairs):
                    last = nc.tensor.transpose(dst[:, i * P:(i + 1) * P], src(i), ident[0:P, 0:P])
                last.then_inc(chain.sem, 1)

            def embed_turn(s):
                EMBED.wait(pe, s, "norm")
                if not (isinstance(s, int) and s == 0):
                    MIX.wait(pe, s - 1, "xt_b")
                turn_pairs(pA, lambda i: xn1[:, 2 * i:2 * i + 2, :].rearrange("p a d -> p (a d)"), PAIRS, EMBED)

            def body(t, par, experts, embed, mix, close):
                new = 1 - par
                s = t + 1
                for u in range(E):
                    if experts:
                        n = t * E + u
                        if u == 0:
                            MIX.wait(pe, t, "xt_b")
                        if not isinstance(n, int) or n >= 2:
                            pe.wait_ge(h_ready, n - 1)
                        for b, (c0, c1) in enumerate(((0, HALF), (HALF, TOK))):
                            for k, w in enumerate((w1hi, w1lo)):
                                last = nc.tensor.matmul(z_of(u)[:, b, 0:c1 - c0], w[:, u, :], xt[par][:, c0:c1],
                                                        start=(k == 0), stop=(k == 1))
                        last.then_inc(z_ready, 1)
                    if mix and u == 0:
                        EMBED.wait(pe, s, "xn1t")
                        if not (isinstance(s, int) and s == 0):
                            MIX.wait(pe, s - 1, "acc")
                        nc.tensor.matmul(pA[:, 0:HALF], wih[:, :], xn1t[:, :], start=True, stop=False)
                        nc.tensor.matmul(pA[:, 0:HALF], whh[:, :], hid[:, :], start=False, stop=True)\
                            .then_inc(MIX.sem, 1)
                    if mix and u == 1:
                        MIX.wait(pe, s, "hid")
                        for i in range(PAIRS):
                            last = nc.tensor.transpose(pB[0:P, i * 2 * D:(i + 1) * 2 * D], hid[:, i * P:(i + 1) * P],
                                                       ident[:, :])
                        last.then_inc(MIX.sem, 1)
                    if embed and u == 3:
                        embed_in(t + 2)
                    if mix and u == 7:
                        MIX.wait(pe, s, "lo")
                        for i in range(PAIRS):
                            last = nc.tensor.transpose(pB[:, i * P:(i + 1) * P],
                                                       x2hl[:, i, :, :].rearrange("p a d -> p (a d)"), ident[0:P, 0:P])
                        last.then_inc(MIX.sem, 1)
                        if embed:
                            pe.wait_ge(h1_kept, t + 3)
                        for i in range(PAIRS, TILES):
                            last = nc.tensor.transpose(pA[:, (i - PAIRS) * P:(i - PAIRS + 1) * P],
                                                       x2hl[:, i, :, :].rearrange("p a d -> p (a d)"), ident[0:P, 0:P])
                        last.then_inc(MIX.sem, 1)
                    if mix and u == 9:
                        MIX.wait(pe, s, "xt_b")
                        for i in range(TILES):
                            for k, w in enumerate((gwhi, gwlo)):
                                last = nc.tensor.matmul(pB[0:P, i * E:(i + 1) * E], xt[new][:, i * P:(i + 1) * P],
                                                        w[:, :], start=(k == 0), stop=(k == 1))
                        last.then_inc(MIX.sem, 1)
                    if embed and u == 12:
                        embed_turn(t + 2)
                    if mix and u == 13:
                        MIX.wait(pe, s, "gates")
                        nc.tensor.transpose(pB[0:P, 0:P], gates[new][:, :, :].rearrange("p i e -> p (i e)"),
                                            ident[0:P, 0:P]).then_inc(MIX.sem, 1)
                    if mix and u == 14:
                        MIX.wait(pe, s, "gt")
                        if embed:
                            EMBED.wait(pe, t + 2, "xn1t")
                        nc.tensor.matmul(pA[0:P, 0:TILES * D], gt[:, :], b2d[:, :, :].rearrange("p i d -> p (i d)"),
                                         start=True, stop=True).then_inc(MIX.sem, 1)
                    if experts:
                        if u >= 1:
                            second(t, u - 1)
                        elif not (isinstance(t, int) and t == 0):
                            second(t - 1, E - 1)

            def second(step, e):
                n = step * E + e
                pe.wait_ge(h_ready, n + 1)
                if not isinstance(n, int) or n >= 2:
                    pe.wait_ge(p_ready, n - 1)
                for i in range(TILES):
                    last = nc.tensor.matmul(tiles_of(pY[e % 2])[:, i, :], hexp[e % 2][:, i * P:(i + 1) * P],
                                            w2s[:, e, :], start=True, stop=True)
                last.then_inc(y_ready, 1)

            embed_in(0)
            embed_turn(0)
            run(pe, body)
            second(STEPS - 1, E - 1)


def kernel(**inputs):
    import numpy as np
    import concourse.bacc as bacc
    from concourse import mybir as mb
    from concourse.bass_utils import run_bass_kernel_spmd

    steps, _, height, width = inputs["x"].shape
    patch = 8
    rows, cols = height // patch, width // patch
    d = inputs["L0_tok_W"].shape[0]
    experts = inputs["L0_ffn_gate_w"].shape[1]
    tiles = 7
    p = rows * cols // tiles

    def a(name):
        return np.asarray(inputs["L0_" + name])

    x = np.asarray(inputs["x"]).reshape(steps, rows, patch, cols, patch).transpose(2, 4, 0, 1, 3)
    x = x.reshape(patch * patch, steps, p, tiles).transpose(0, 1, 3, 2).reshape(patch * patch, -1)
    arrays = {
        "x_in": x, "tok_w": a("tok_W").T, "tok_b": a("tok_b"), "w_ih": a("attn_W_ih").T, "w_hh": a("attn_W_hh").T,
        "b_ih": a("attn_b_ih"), "b_hh": a("attn_b_hh"), "gate_w": a("ffn_gate_w"), "gate_b": a("ffn_gate_b"),
        "w1": a("ffn_w1").transpose(1, 0, 2), "b1": a("ffn_b1").T, "w2": a("ffn_w2").transpose(1, 0, 2),
        "b2": a("ffn_b2"), "gamma": a("ffn_gamma"), "beta": a("ffn_beta"),
    }
    arrays = {k: np.ascontiguousarray(v) for k, v in arrays.items()}
    nc = bacc.Bacc("TRN2", target_bir_lowering=False, num_devices=1)
    args = [nc.dram_tensor(k, v.shape, mb.dt.from_np(v.dtype), kind="ExternalInput").ap() for k, v in arrays.items()]
    out = nc.dram_tensor("out", (steps, p, tiles, d), mb.dt.float32, kind="ExternalOutput").ap()
    vit_tower_kernel(nc, *args, out)
    r = run_bass_kernel_spmd(nc, [arrays], core_ids=[0])
    return r.results[0]["out"].reshape(steps, rows * cols, d)
```

```python
import concourse.bass as bass
from concourse import mybir
from contextlib import ExitStack


def vit_tower_kernel(nc, x_in, tok_w, tok_b, w_ih, w_hh, b_ih, b_hh, gate_w, gate_b,
                     w1, b1, w2, b2, gamma, beta, out):
    f32 = mybir.dt.float32
    f32r = mybir.dt.float32r
    i32 = mybir.dt.int32
    ALU = mybir.AluOpType
    ACT = mybir.ActivationFunctionType
    X = mybir.AxisListType.X

    D = w_ih.shape[0]
    STEPS = out.shape[0]
    P = out.shape[1]
    TILES = out.shape[2]
    TOK = P * TILES
    HALF = TOK // 2
    E = w1.shape[1]
    Q = E // 2
    F = w1.shape[2]
    K_IN = tok_w.shape[0]
    PAIRS = (TILES + 1) // 2
    EVEN = 2 * PAIRS
    FIRST = P * PAIRS
    REST = TOK - FIRST
    EPS = 1e-5
    FAR = -1.0e30
    RING = 4
    PARTS = 2
    assert 2 * D == 128 and F == 128 and FIRST <= 512 and HALF <= 512 and EVEN * D <= 512
    assert Q % RING == 0 and (STEPS - 4) % 2 == 0

    gates_dram = nc.dram_tensor("gates_dram", (STEPS, E, TOK), f32)
    h2_dram = nc.dram_tensor("h2_dram", (STEPS, P, TILES, D), f32)

    ctx = ExitStack()
    with ctx:
        def sb(name, shape, dt=f32):
            return ctx.enter_context(nc.sbuf_tensor(name, shape, dt))

        def ps(name, banks):
            return ctx.enter_context(nc.psum_tensor(name, [128, 512 * banks], f32))

        def sem(name):
            return ctx.enter_context(nc.semaphore(name))

        tokw = sb("tokw", [K_IN + 1, D])
        wih = sb("wih", [2 * D, 2 * D])
        whh = sb("whh", [2 * D, 2 * D])
        rbias = sb("rbias", [2 * D, 2])
        rb = sb("rb", [2 * D, 1])
        w1f = sb("w1f", [2 * D, E, F])
        w1hi = sb("w1hi", [2 * D, E, F], f32r)
        w1lo = sb("w1lo", [2 * D, E, F], f32r)
        gwf = sb("gwf", [2 * D, E])
        gwhi = sb("gwhi", [2 * D, E], f32r)
        gwlo = sb("gwlo", [2 * D, E], f32r)
        b1c = sb("b1c", [F, E])
        w2s = sb("w2s", [F, E, D])
        b2c = sb("b2c", [2 * D, Q])
        gbias = sb("gbias", [P, E])
        gam = sb("gam", [P, D])
        bet = sb("bet", [P, D])
        ident = sb("ident", [128, 128])
        fold = sb("fold", [2 * D, D])
        rank_i = sb("rank_i", [P, E], i32)
        rank = sb("rank", [P, E])
        nhalf = sb("nhalf", [P, TILES])

        xcur = sb("xcur", [K_IN + 1, TOK])
        h1 = sb("h1", [P, TILES, D])
        cen1 = sb("cen1", [P, TILES, D])
        sq1 = sb("sq1", [P, TILES, D])
        st1 = sb("st1", [P, 4, TILES])
        xn1 = sb("xn1", [P, EVEN, D])
        xn1t = sb("xn1t", [2 * D, FIRST])
        hid = sb("hid", [2 * D, FIRST])
        h2 = sb("h2", [P, TILES, D])
        cen2 = sb("cen2", [P, TILES, D])
        sq2 = sb("sq2", [P, TILES, D])
        st2 = sb("st2", [P, 4, TILES])
        x2 = sb("x2", [P, TILES, D])
        x2hl = sb("x2hl", [P, TILES, 2, D], f32r)
        xt = [sb(f"xt{i}", [2 * D, TOK], f32r) for i in range(2)]
        lg = sb("lg", [P, TILES, E])
        hit = sb("hit", [P, TILES, E])
        best = [sb(f"best{i}", [P, TILES, E]) for i in range(2)]
        tv = sb("tv", [P, 9, TILES])
        gates = sb("gates", [P, TILES, E])
        gt = sb("gt", [E, TOK])
        spread = [sb(f"spread{i}", [2 * D, Q, TOK]) for i in range(2)]
        hexp = [sb(f"hexp{i}", [F, TOK]) for i in range(RING)]
        prod = [sb(f"prod{i}", [2 * D, TOK]) for i in range(RING)]
        acc = [sb(f"acc{i}", [2 * D, TOK]) for i in range(2)]
        cen3 = sb("cen3", [P, TILES, D])
        sq3 = sb("sq3", [P, TILES, D])
        st3 = sb("st3", [P, 4, TILES])
        h2c = sb("h2c", [P, TILES, D])
        h2b = sb("h2b", [P, TILES, D])
        yn = sb("yn", [P, TILES, D])
        yo = sb("yo", [P, TILES, D])

        pZ = [ps(f"pZ{i}", 2) for i in range(2)]
        pO = ps("pO", 2)
        pA = ps("pA", 1)
        pB = ps("pB", 1)

        class Chain:

            def __init__(self, name, stages):
                self.sem, self.stages = sem(name), stages.split()

            def wait(self, eng, step, stage):
                eng.wait_ge(self.sem, step * len(self.stages) + self.stages.index(stage) + 1)

        EMBED = Chain("embed_stage", "h1 sum center square sumsq var rstd norm turned xn1t")
        MIX = Chain("mix_stage", "pre hid hid_turned h2 sum center square sumsq var rstd x2 hi lo "
                                 "turned_a turned_b xt_a xt_b")
        GATE = Chain("gate_stage", "logits biased max1 hit1 ranked1 first1 best1 without "
                                   "max2 hit2 ranked2 first2 best2 diff exp den p1 p2 g1 g2 gates "
                                   "turned_a turned_b gt_a gt_b")
        CLOSE = Chain("close_stage", "y sum center square sumsq var rstd norm gamma out")

        wload = sem("weights_loaded")
        xload = sem("x_loaded")
        consts = sem("constants_set")
        dve_consts = sem("split_weights_set")
        h1_kept = sem("h1_kept")
        h2_stored = sem("h2_stored")
        h2_loaded = sem("h2_loaded")
        h2b_set = sem("h2b_set")
        gt_stored = sem("gates_stored")
        spread_in = sem("spread_loaded")
        z_ready = sem("z_ready")
        h_ready = sem("h_ready")
        y_ready = sem("y_ready")
        p_ready = sem("product_ready")
        summed = sem("product_summed")
        stored = sem("out_stored")

        def halves(tensor):
            return tensor[:, :].rearrange("p (b c) -> p b c", b=2)[:, :, 0:HALF]

        def tiles_of(bank):
            return bank[0:P, 0:TILES * D].rearrange("p (i d) -> p i d", d=D)

        def over_d(ap):
            return ap.unsqueeze(2).to_broadcast([P, TILES, D])

        def over_e(ap):
            return ap.unsqueeze(2).to_broadcast([P, TILES, E])

        def over_tiles(ap, n):
            return ap.unsqueeze(1).to_broadcast([P, TILES, n])

        def known(value, bound):
            return isinstance(value, int) and value < bound

        def run(eng, body):
            body(-2, 0, mix=True, embed=True)
            body(-1, 1, gate=True, mix=True, embed=True)
            body(0, 0, experts=True, gate=True, mix=True, embed=True)
            with eng.Fori(0, (STEPS - 4) // 2) as i:
                t = 2 * i + 1
                body(t, 1, experts=True, gate=True, mix=True, embed=True, close=True)
                body(t + 1, 0, experts=True, gate=True, mix=True, embed=True, close=True)
            body(STEPS - 3, 1, experts=True, gate=True, mix=True, close=True)
            body(STEPS - 2, 0, experts=True, gate=True, close=True)
            body(STEPS - 1, 1, experts=True, close=True)

        block = ctx.enter_context(nc.Block())

        loads = [(tokw[0:K_IN, :], tok_w), (tokw[K_IN:K_IN + 1, :], tok_b.unsqueeze(0))]
        for k in range(2):
            rows = slice(k * D, (k + 1) * D)
            loads += [(wih[rows, rows], w_ih), (whh[rows, rows], w_hh),
                      (rbias[rows, 0:1], b_ih.unsqueeze(1)), (rbias[rows, 1:2], b_hh.unsqueeze(1)),
                      (gwf[rows, :], gate_w), (w1f[rows, :, :], w1)]
        loads += [(b1c[:, :], b1), (w2s[:, :, :], w2), (b2c[:, :], b2),
                  (gbias[:, :], gate_b.partition_broadcast(P)), (gam[:, :], gamma.partition_broadcast(P)),
                  (bet[:, :], beta.partition_broadcast(P))]
        W_LOADED = 16 * len(loads)
        FILLS = 8

        @block.sync
        def _(sp):
            def load_x(s):
                if not known(s, 1):
                    EMBED.wait(sp, s - 1, "h1")
                sp.dma_start(xcur[0:K_IN, :], x_in[:, bass.ds(s * TOK, TOK)]).then_inc(xload, 16)

            def keep_h2(s):
                MIX.wait(sp, s, "h2")
                sp.dma_start(h2_dram[bass.ds(s, 1), :, :, :].rearrange("s p i d -> (s p) i d"),
                             h2[:, :, :]).then_inc(h2_stored, 16)

            def fetch_h2(s):
                sp.wait_ge(h2_stored, 16 * s + 16)
                if not known(s, 1):
                    sp.wait_ge(h2b_set, s)
                sp.dma_start(h2c[:, :, :], h2_dram[bass.ds(s, 1), :, :, :].rearrange("s p i d -> (s p) i d"))\
                    .then_inc(h2_loaded, 16)

            def spread_gates(s, par):
                GATE.wait(sp, s, "gt_b")
                sp.dma_start(gates_dram[bass.ds(s, 1), :, :].rearrange("s e n -> (s e) n"), gt[:, :])\
                    .then_inc(gt_stored, 16)
                sp.wait_ge(gt_stored, 16 * s + 16)
                if not known(s, 2):
                    sp.wait_ge(p_ready, (s - 1) * 2 * Q)
                for part in range(PARTS):
                    for k in range(2):
                        q0, n = part * (Q // PARTS), Q // PARTS
                        src = gates_dram[bass.ds(s, 1), :, :].rearrange("s (q k) n -> k s q n", k=2)[k]
                        sp.dma_start(spread[par][k * D:(k + 1) * D, q0:q0 + n, :],
                                     src[:, q0:q0 + n, :].to_broadcast([D, n, TOK])).then_inc(spread_in, 16)

            def store(s):
                CLOSE.wait(sp, s, "out")
                sp.dma_start(out[bass.ds(s, 1), :, :, :].rearrange("s p i d -> (s p) i d"), yo[:, :, :])\
                    .then_inc(stored, 16)

            def body(t, par, experts=False, gate=False, mix=False, embed=False, close=False):
                if embed:
                    load_x(t + 3)
                if close:
                    fetch_h2(t - 1)
                if mix:
                    keep_h2(t + 2)
                if gate:
                    spread_gates(t + 1, 1 - par)
                if close:
                    store(t - 1)

            load_x(0)
            sp.wait_ge(consts, FILLS)
            for dst, src in loads:
                sp.dma_start(dst, src).then_inc(wload, 16)
            run(sp, body)
            fetch_h2(STEPS - 1)
            store(STEPS - 1)
            sp.wait_ge(stored, 16 * STEPS)

        @block.gpsimd
        def _(pool):
            zeros = [wih[:, :], whh[:, :], xn1[:, :, :], hid[:, :], ident[:, :], fold[:, :]]
            fills = [(z, 0.0) for z in zeros] + [(nhalf[:, :], -0.5), (xcur[K_IN:K_IN + 1, :], 1.0)]
            for k, (dst, value) in enumerate(fills):
                if k:
                    pool.wait_ge(consts, k)
                nc.gpsimd.memset(dst, value).then_inc(consts, 1)
            pool.wait_ge(consts, FILLS)
            nc.gpsimd.iota(rank_i[:, :], pattern=[[-1, E]], base=E, channel_multiplier=0).then_inc(consts, 1)
            pool.wait_ge(consts, FILLS + 1)
            nc.gpsimd.affine_select(out=ident[:, :], in_=ident[:, :], compare_op=ALU.not_equal, fill=1.0,
                                    base=0, pattern=[[-1, 128]], channel_multiplier=1).then_inc(consts, 1)
            for k in range(2):
                pool.wait_ge(consts, FILLS + 2 + k)
                nc.gpsimd.affine_select(out=fold[:, :], in_=fold[:, :], compare_op=ALU.not_equal, fill=1.0,
                                        base=-k * D, pattern=[[-1, D]], channel_multiplier=1).then_inc(consts, 1)
            pool.wait_ge(wload, W_LOADED)

            def rstd(chain, s, st):
                chain.wait(pool, s, "var")
                nc.gpsimd.tensor_tensor(st[:, 3, :], st[:, 2, :], nhalf[:, :], ALU.pow).then_inc(chain.sem, 1)

            def add(step, q, par):
                n = step * Q + q
                pool.wait_ge(p_ready, 2 * n + 2)
                if q == 0:
                    MIX.wait(pool, step, "xt_b")
                    sofar = xt[par][:, :].bitcast(f32)
                else:
                    pool.wait_ge(summed, n)
                    sofar = acc[par][:, :]
                nc.gpsimd.tensor_tensor(acc[par][:, :], sofar, prod[q % RING][:, :], ALU.add).then_inc(summed, 1)

            def add_beta(s):
                pool.wait_ge(h2_loaded, 16 * s + 16)
                if not known(s, 1):
                    CLOSE.wait(pool, s - 1, "out")
                nc.gpsimd.tensor_tensor(h2b[:, :, :], h2c[:, :, :], over_tiles(bet[:, :], D), ALU.add)\
                    .then_inc(h2b_set, 1)

            def body(t, par, experts=False, gate=False, mix=False, embed=False, close=False):
                for u in range(E):
                    if experts and u % 2 == 1:
                        if u > 1:
                            add(t, u // 2 - 1, par)
                        elif not known(t, 1):
                            add(t - 1, Q - 1, 1 - par)
                    if close and u == 2:
                        add_beta(t - 1)
                    if mix and u == 8:
                        rstd(MIX, t + 2, st2)
                    if close and u == 9:
                        rstd(CLOSE, t - 1, st3)
                    if embed and u == 10:
                        rstd(EMBED, t + 3, st1)

            rstd(EMBED, 0, st1)
            run(pool, body)
            add(STEPS - 1, Q - 1, (STEPS - 1) % 2)
            add_beta(STEPS - 1)
            rstd(CLOSE, STEPS - 1, st3)

        @block.scalar
        def _(act):
            act.wait_ge(wload, W_LOADED)
            nc.scalar.activation(w1hi[:, :, :], w1f[:, :, :], ACT.Copy).then_inc(dve_consts, 1)
            nc.scalar.activation(gwhi[:, :], gwf[:, :], ACT.Copy).then_inc(dve_consts, 1)

            def keep_h1(s):
                EMBED.wait(act, s, "h1")
                if not known(s, 1):
                    MIX.wait(act, s - 1, "h2")
                nc.scalar.activation(h1[:, :, :], tiles_of(pA), ACT.Copy).then_inc(h1_kept, 1)

            def square(chain, s, dst, src):
                chain.wait(act, s, "center")
                nc.scalar.activation(dst[:, :, :], src[:, :, :], ACT.Square).then_inc(chain.sem, 1)

            def keep_xn1t(s):
                EMBED.wait(act, s, "turned")
                if not known(s, 1):
                    MIX.wait(act, s - 1, "pre")
                nc.scalar.activation(xn1t[:, :], pB[:, 0:FIRST], ACT.Copy).then_inc(EMBED.sem, 1)

            def body(t, par, experts=False, gate=False, mix=False, embed=False, close=False):
                for u in range(E):
                    if experts:
                        n = t * E + u
                        act.wait_ge(z_ready, n + 1)
                        if not known(n, RING):
                            act.wait_ge(y_ready, t * E + 2 * (u // 2) - RING + 2)
                        nc.scalar.activation(hexp[u % RING][:, :].rearrange("p (b c) -> p b c", b=2),
                                             halves(pZ[u % 2]), ACT.Relu, bias=b1c[:, u:u + 1])\
                            .then_inc(h_ready, 1)
                    if mix and u == 0:
                        MIX.wait(act, t + 2, "pre")
                        nc.scalar.activation(hid[:, :], pA[:, 0:FIRST], ACT.Tanh, bias=rb[:, 0:1])\
                            .then_inc(MIX.sem, 1)
                    if mix and u == 5:
                        square(MIX, t + 2, sq2, cen2)
                    if embed and u == 5:
                        keep_h1(t + 3)
                    if close and u == 6:
                        square(CLOSE, t - 1, sq3, cen3)
                    if gate and u == 7:
                        GATE.wait(act, t + 1, "diff")
                        nc.scalar.activation(tv[:, 5, :], tv[:, 4, :], ACT.Exp).then_inc(GATE.sem, 1)
                    if embed and u == 8:
                        square(EMBED, t + 3, sq1, cen1)
                    if mix and u == 10:
                        MIX.wait(act, t + 2, "x2")
                        nc.scalar.activation(x2hl[:, :, 0, :], x2[:, :, :], ACT.Copy).then_inc(MIX.sem, 1)
                    if gate and u == 11:
                        GATE.wait(act, t + 1, "turned_b")
                        if not known(t, 0):
                            act.wait_ge(gt_stored, 16 * t + 16)
                        nc.scalar.activation(gt[:, 0:FIRST], pB[0:E, 0:FIRST], ACT.Copy).then_inc(GATE.sem, 1)
                    if embed and u == 13:
                        keep_xn1t(t + 3)
                if mix:
                    MIX.wait(act, t + 2, "turned_b")
                    if experts:
                        act.wait_ge(z_ready, t * E + E)
                        act.wait_ge(summed, t * Q + 1)
                    nc.scalar.activation(xt[par][:, 0:FIRST], pA[:, 0:FIRST], ACT.Copy).then_inc(MIX.sem, 1)

            keep_h1(0)
            square(EMBED, 0, sq1, cen1)
            keep_xn1t(0)
            act.wait_ge(dve_consts, 4)
            run(act, body)
            square(CLOSE, STEPS - 1, sq3, cen3)

        @block.vector
        def _(dve):
            dve.wait_ge(wload, W_LOADED)
            dve.wait_ge(dve_consts, 2)
            nc.vector.tensor_tensor(w1lo[:, :, :], w1f[:, :, :], w1hi[:, :, :].bitcast(f32), ALU.subtract)\
                .then_inc(dve_consts, 1)
            nc.vector.tensor_tensor(rb[:, :], rbias[:, 0:1], rbias[:, 1:2], ALU.add).then_inc(dve_consts, 1)
            nc.vector.tensor_tensor(gwlo[:, :], gwf[:, :], gwhi[:, :].bitcast(f32), ALU.subtract)\
                .then_inc(dve_consts, 1)
            dve.wait_ge(consts, FILLS + 2)
            nc.vector.tensor_copy(rank[:, :], rank_i[:, :]).then_inc(dve_consts, 1)
            dve.wait_ge(dve_consts, 6)

            def norm_center(chain, s, src, st, cen):
                nc.vector.tensor_reduce(st[:, 0, :], src, X, ALU.add).then_inc(chain.sem, 1)
                chain.wait(dve, s, "sum")
                nc.vector.scalar_tensor_tensor(out=cen[:, :, :], in0=over_d(st[:, 0, :]), scalar=-1.0 / D,
                                               in1=src, op0=ALU.mult, op1=ALU.add).then_inc(chain.sem, 1)

            def norm_var(chain, s, sq, st):
                chain.wait(dve, s, "square")
                nc.vector.tensor_reduce(st[:, 1, :], sq[:, :, :], X, ALU.add).then_inc(chain.sem, 1)
                chain.wait(dve, s, "sumsq")
                nc.vector.tensor_scalar(st[:, 2, :], st[:, 1, :], 1.0 / D, EPS, ALU.mult, ALU.add)\
                    .then_inc(chain.sem, 1)

            def norm_scale(chain, s, cen, st, dst):
                chain.wait(dve, s, "rstd")
                nc.vector.tensor_tensor(dst, cen[:, :, :], over_d(st[:, 3, :]), ALU.mult).then_inc(chain.sem, 1)

            def embed_center(s):
                dve.wait_ge(h1_kept, s + 1)
                norm_center(EMBED, s, h1[:, :, :], st1, cen1)

            def embed_norm(s):
                norm_scale(EMBED, s, cen1, st1, xn1[:, 0:TILES, :])

            def bias_logits(s):
                GATE.wait(dve, s, "logits")
                nc.vector.tensor_tensor(lg[:, :, :], pB[0:P, 0:TILES * E].rearrange("p (i e) -> p i e", e=E),
                                        over_tiles(gbias[:, :], E), ALU.add).then_inc(GATE.sem, 1)

            def find(s, k):
                top, mark, one = tv[:, k, :], tv[:, 2 + k, :], best[k]
                GATE.wait(dve, s, "without" if k else "biased")
                nc.vector.tensor_reduce(top, lg[:, :, :], X, ALU.max).then_inc(GATE.sem, 1)
                GATE.wait(dve, s, f"max{k + 1}")
                nc.vector.tensor_tensor(hit[:, :, :], lg[:, :, :], over_e(top), ALU.is_equal).then_inc(GATE.sem, 1)
                GATE.wait(dve, s, f"hit{k + 1}")
                nc.vector.tensor_tensor(hit[:, :, :], hit[:, :, :], over_tiles(rank[:, :], E), ALU.mult)\
                    .then_inc(GATE.sem, 1)
                GATE.wait(dve, s, f"ranked{k + 1}")
                nc.vector.tensor_reduce(mark, hit[:, :, :], X, ALU.max).then_inc(GATE.sem, 1)
                GATE.wait(dve, s, f"first{k + 1}")
                nc.vector.tensor_tensor(one[:, :, :], hit[:, :, :], over_e(mark), ALU.is_equal).then_inc(GATE.sem, 1)

            def find_first(s):
                find(s, 0)
                GATE.wait(dve, s, "best1")
                nc.vector.scalar_tensor_tensor(out=lg[:, :, :], in0=best[0][:, :, :], scalar=FAR, in1=lg[:, :, :],
                                               op0=ALU.mult, op1=ALU.add).then_inc(GATE.sem, 1)

            def find_second(s):
                find(s, 1)
                nc.vector.tensor_tensor(tv[:, 4, :], tv[:, 1, :], tv[:, 0, :], ALU.subtract).then_inc(GATE.sem, 1)

            def gate_weights(s):
                GATE.wait(dve, s, "exp")
                nc.vector.tensor_scalar(tv[:, 6, :], tv[:, 5, :], 1.0, None, ALU.add).then_inc(GATE.sem, 1)
                GATE.wait(dve, s, "den")
                nc.vector.reciprocal(tv[:, 7, :], tv[:, 6, :]).then_inc(GATE.sem, 1)
                GATE.wait(dve, s, "p1")
                nc.vector.tensor_tensor(tv[:, 8, :], tv[:, 5, :], tv[:, 7, :], ALU.mult).then_inc(GATE.sem, 1)
                GATE.wait(dve, s, "p2")
                nc.vector.tensor_tensor(best[0][:, :, :], best[0][:, :, :], over_e(tv[:, 7, :]), ALU.mult)\
                    .then_inc(GATE.sem, 1)
                nc.vector.tensor_tensor(best[1][:, :, :], best[1][:, :, :], over_e(tv[:, 8, :]), ALU.mult)\
                    .then_inc(GATE.sem, 1)
                GATE.wait(dve, s, "g2")
                nc.vector.tensor_tensor(gates[:, :, :], best[0][:, :, :], best[1][:, :, :], ALU.add)\
                    .then_inc(GATE.sem, 1)

            def product(step, q, par):
                n = step * Q + q
                if q == 0:
                    dve.wait_ge(spread_in, (step + 1) * 2 * PARTS * 16)
                if not known(n, RING):
                    dve.wait_ge(summed, n - RING + 1)
                for b in range(2):
                    dve.wait_ge(y_ready, 2 * n + b + 1)
                    nc.vector.scalar_tensor_tensor(
                        out=prod[q % RING][:, b * HALF:(b + 1) * HALF], in0=halves(pO)[:, b, :],
                        scalar=b2c[:, q:q + 1], in1=spread[par][:, q, b * HALF:(b + 1) * HALF],
                        op0=ALU.add, op1=ALU.mult).then_inc(p_ready, 1)

            def close_center(s):
                CLOSE.wait(dve, s, "y")
                norm_center(CLOSE, s, tiles_of(pB), st3, cen3)

            def close_gamma(s):
                norm_scale(CLOSE, s, cen3, st3, yn[:, :, :])
                CLOSE.wait(dve, s, "norm")
                nc.vector.tensor_tensor(yn[:, :, :], yn[:, :, :], over_tiles(gam[:, :], D), ALU.mult)\
                    .then_inc(CLOSE.sem, 1)

            def close_out(s):
                CLOSE.wait(dve, s, "gamma")
                dve.wait_ge(h2b_set, s + 1)
                if not known(s, 1):
                    dve.wait_ge(stored, 16 * s)
                nc.vector.tensor_tensor(yo[:, :, :], yn[:, :, :], h2b[:, :, :], ALU.add).then_inc(CLOSE.sem, 1)

            def body(t, par, experts=False, gate=False, mix=False, embed=False, close=False):
                g, s, a, c = t + 1, t + 2, t + 3, t - 1
                for u in range(E):
                    if experts and u % 2 == 1:
                        if u > 1:
                            product(t, u // 2 - 1, par)
                        elif not known(t, 1):
                            product(t - 1, Q - 1, 1 - par)
                    if gate and u == 1:
                        bias_logits(g)
                    if gate and u == 2:
                        find_first(g)
                    if mix and u == 3:
                        MIX.wait(dve, s, "hid_turned")
                        dve.wait_ge(h1_kept, s + 1)
                        if not known(s, 1):
                            dve.wait_ge(h2_stored, 16 * s)
                        nc.vector.tensor_tensor(h2[:, :, :], tiles_of(pA), h1[:, :, :], ALU.add)\
                            .then_inc(MIX.sem, 1)
                    if mix and u == 4:
                        MIX.wait(dve, s, "h2")
                        norm_center(MIX, s, h2[:, :, :], st2, cen2)
                    if close and u == 5:
                        close_center(c)
                    if gate and u == 6:
                        find_second(g)
                    if embed and u == 7:
                        embed_center(a)
                    if mix and u == 7:
                        norm_var(MIX, s, sq2, st2)
                    if gate and u == 8:
                        gate_weights(g)
                    if close and u == 8:
                        norm_var(CLOSE, c, sq3, st3)
                    if embed and u == 9:
                        norm_var(EMBED, a, sq1, st1)
                    if mix and u == 10:
                        norm_scale(MIX, s, cen2, st2, x2[:, :, :])
                        MIX.wait(dve, s, "hi")
                        nc.vector.tensor_tensor(x2hl[:, :, 1, :], x2[:, :, :], x2hl[:, :, 0, :].bitcast(f32),
                                                ALU.subtract).then_inc(MIX.sem, 1)
                    if gate and u == 11:
                        GATE.wait(dve, g, "turned_b")
                        if not known(g, 1):
                            dve.wait_ge(gt_stored, 16 * g)
                        nc.vector.tensor_copy(gt[:, FIRST:TOK], pA[0:E, 0:REST]).then_inc(GATE.sem, 1)
                    if embed and u == 11:
                        embed_norm(a)
                    if close and u == 12:
                        close_gamma(c)
                    if close and u == 14:
                        close_out(c)
                if mix:
                    MIX.wait(dve, s, "turned_b")
                    if experts:
                        dve.wait_ge(z_ready, t * E + E)
                        dve.wait_ge(summed, t * Q + 1)
                    nc.vector.tensor_copy(xt[par][:, FIRST:TOK], pB[:, 0:REST]).then_inc(MIX.sem, 1)

            embed_center(0)
            norm_var(EMBED, 0, sq1, st1)
            embed_norm(0)
            run(dve, body)
            last = STEPS - 1
            product(last, Q - 1, last % 2)
            close_center(last)
            norm_var(CLOSE, last, sq3, st3)
            close_gamma(last)
            close_out(last)

        @block.tensor
        def _(pe):
            pe.wait_ge(wload, W_LOADED)
            pe.wait_ge(consts, FILLS + 4)
            pe.wait_ge(dve_consts, 6)

            def embed_in(s):
                pe.wait_ge(xload, 16 * s + 16)
                if not known(s, 1):
                    MIX.wait(pe, s - 1, "h2")
                for i in range(TILES):
                    last = nc.tensor.matmul(tiles_of(pA)[:, i, :], xcur[:, i * P:(i + 1) * P], tokw[:, :],
                                            start=True, stop=True)
                last.then_inc(EMBED.sem, 1)

            def embed_turn(s):
                EMBED.wait(pe, s, "norm")
                if not known(s, 2):
                    GATE.wait(pe, s - 2, "gt_b")
                for i in range(PAIRS):
                    last = nc.tensor.transpose(pB[:, i * P:(i + 1) * P],
                                               xn1[:, 2 * i:2 * i + 2, :].rearrange("p a d -> p (a d)"),
                                               ident[0:P, 0:P])
                last.then_inc(EMBED.sem, 1)

            def recur(s):
                EMBED.wait(pe, s, "xn1t")
                if not known(s, 1):
                    MIX.wait(pe, s - 1, "xt_b")
                nc.tensor.matmul(pA[:, 0:FIRST], wih[:, :], xn1t[:, :], start=True, stop=False)
                nc.tensor.matmul(pA[:, 0:FIRST], whh[:, :], hid[:, :], start=False, stop=True).then_inc(MIX.sem, 1)

            def hidden_turn(s):
                MIX.wait(pe, s, "hid")
                for i in range(PAIRS):
                    last = nc.tensor.transpose(pA[0:P, i * 2 * D:(i + 1) * 2 * D], hid[:, i * P:(i + 1) * P],
                                               ident[:, :])
                last.then_inc(MIX.sem, 1)

            def x2_turn(s, embed, gate):
                MIX.wait(pe, s, "lo")
                if gate:
                    GATE.wait(pe, s - 1, "gt_b")
                if embed:
                    EMBED.wait(pe, s + 1, "xn1t")
                for bank, first, end in ((pA, 0, PAIRS), (pB, PAIRS, TILES)):
                    for i in range(first, end):
                        last = nc.tensor.transpose(bank[:, (i - first) * P:(i - first + 1) * P],
                                                   x2hl[:, i, :, :].bitcast(f32).rearrange("p a d -> p (a d)"),
                                                   ident[0:P, 0:P])
                    last.then_inc(MIX.sem, 1)

            def logits(s, par):
                MIX.wait(pe, s, "xt_b")
                for i in range(TILES):
                    for k, w in enumerate((gwhi, gwlo)):
                        last = nc.tensor.matmul(pB[0:P, i * E:(i + 1) * E], xt[par][:, i * P:(i + 1) * P], w[:, :],
                                                start=(k == 0), stop=(k == 1))
                last.then_inc(GATE.sem, 1)

            def gates_turn(s, embed, mix, close):
                GATE.wait(pe, s, "gates")
                if close:
                    CLOSE.wait(pe, s - 2, "center")
                if embed:
                    pe.wait_ge(h1_kept, s + 3)
                elif mix:
                    MIX.wait(pe, s + 1, "h2")
                for bank, first, end in ((pB, 0, PAIRS), (pA, PAIRS, TILES)):
                    for i in range(first, end):
                        last = nc.tensor.transpose(bank[0:E, (i - first) * P:(i - first + 1) * P], gates[:, i, :],
                                                   ident[0:P, 0:P])
                    last.then_inc(GATE.sem, 1)

            def first_layer(t, e, par):
                n = t * E + e
                if e == 0:
                    MIX.wait(pe, t, "xt_b")
                if not known(n, 2):
                    pe.wait_ge(h_ready, n - 1)
                for b in range(2):
                    for k, w in enumerate((w1hi, w1lo)):
                        last = nc.tensor.matmul(halves(pZ[e % 2])[:, b, :], w[:, e, :],
                                                xt[par][:, b * HALF:(b + 1) * HALF], start=(k == 0), stop=(k == 1))
                last.then_inc(z_ready, 1)

            def second_layer(t, q):
                n = t * Q + q
                pe.wait_ge(h_ready, 2 * n + 2)
                for b in range(2):
                    if not known(n, 1):
                        pe.wait_ge(p_ready, 2 * n - 1 + b)
                    for k in range(2):
                        e = 2 * q + k
                        last = nc.tensor.matmul(halves(pO)[k * D:(k + 1) * D, b, :], w2s[:, e, :],
                                                hexp[e % RING][:, b * HALF:(b + 1) * HALF], start=True, stop=True)
                    last.then_inc(y_ready, 1)

            def sum_turn(s, par, gate):
                pe.wait_ge(summed, s * Q + Q)
                if gate:
                    GATE.wait(pe, s + 2, "biased")
                for i in range(TILES):
                    last = nc.tensor.matmul(tiles_of(pB)[:, i, :], acc[par][:, i * P:(i + 1) * P], fold[:, :],
                                            start=True, stop=True)
                last.then_inc(CLOSE.sem, 1)

            def body(t, par, experts=False, gate=False, mix=False, embed=False, close=False):
                for u in range(E):
                    if experts:
                        first_layer(t, u, par)
                    if mix and u == 0:
                        recur(t + 2)
                    if gate and u == 1:
                        logits(t + 1, 1 - par)
                    if mix and u == 2:
                        hidden_turn(t + 2)
                    if close and u == 4:
                        sum_turn(t - 1, 1 - par, gate)
                    if embed and u == 5:
                        embed_in(t + 3)
                    if gate and u == 10:
                        gates_turn(t + 1, embed, mix, close)
                    if embed and u == 12:
                        embed_turn(t + 3)
                    if mix and u == 14:
                        x2_turn(t + 2, embed, gate)
                    if experts and u % 2 == 1:
                        if u > 1:
                            second_layer(t, u // 2 - 1)
                        elif not known(t, 1):
                            second_layer(t - 1, Q - 1)

            embed_in(0)
            embed_turn(0)
            run(pe, body)
            second_layer(STEPS - 1, Q - 1)
            sum_turn(STEPS - 1, (STEPS - 1) % 2, False)


def kernel(**inputs):
    import numpy as np
    import concourse.bacc as bacc
    from concourse import mybir as mb
    from concourse.bass_utils import run_bass_kernel_spmd

    steps, _, height, width = inputs["x"].shape
    patch = 8
    rows, cols = height // patch, width // patch
    d = inputs["L0_tok_W"].shape[0]
    tiles = 7
    p = rows * cols // tiles

    def a(name):
        return np.asarray(inputs["L0_" + name])

    x = np.asarray(inputs["x"]).reshape(steps, rows, patch, cols, patch).transpose(2, 4, 0, 1, 3)
    x = x.reshape(patch * patch, steps, p, tiles).transpose(0, 1, 3, 2).reshape(patch * patch, -1)
    arrays = {
        "x_in": x, "tok_w": a("tok_W").T, "tok_b": a("tok_b"), "w_ih": a("attn_W_ih").T, "w_hh": a("attn_W_hh").T,
        "b_ih": a("attn_b_ih"), "b_hh": a("attn_b_hh"), "gate_w": a("ffn_gate_w"), "gate_b": a("ffn_gate_b"),
        "w1": a("ffn_w1").transpose(1, 0, 2), "b1": a("ffn_b1").T, "w2": a("ffn_w2").transpose(1, 0, 2),
        "b2": a("ffn_b2").reshape(-1, 2, d).transpose(1, 2, 0).reshape(2 * d, -1), "gamma": a("ffn_gamma"), "beta": a("ffn_beta"),
    }
    arrays = {k: np.ascontiguousarray(v) for k, v in arrays.items()}
    nc = bacc.Bacc("TRN2", target_bir_lowering=False, num_devices=1)
    args = [nc.dram_tensor(k, v.shape, mb.dt.from_np(v.dtype), kind="ExternalInput").ap() for k, v in arrays.items()]
    out = nc.dram_tensor("out", (steps, p, tiles, d), mb.dt.float32, kind="ExternalOutput").ap()
    vit_tower_kernel(nc, *args, out)
    r = run_bass_kernel_spmd(nc, [arrays], core_ids=[0])
    return r.results[0]["out"].reshape(steps, rows * cols, d)
```

```python
import concourse.bass as bass
from concourse import mybir
from contextlib import ExitStack


def vit_tower_kernel(nc, x_in, tok_w, tok_b, w_ih, w_hh, b_ih, b_hh, gate_w, gate_b,
                     w1, b1, w2, b2, gamma, beta, out):
    f32 = mybir.dt.float32
    f32r = mybir.dt.float32r
    i32 = mybir.dt.int32
    ALU = mybir.AluOpType
    ACT = mybir.ActivationFunctionType
    X = mybir.AxisListType.X

    D = w_ih.shape[0]
    STEPS = out.shape[0]
    P = out.shape[1]
    TILES = out.shape[2]
    TOK = P * TILES
    HALF = TOK // 2
    E = w1.shape[1]
    Q = E // 2
    F = w1.shape[2]
    K_IN = tok_w.shape[0]
    PAIRS = (TILES + 1) // 2
    EVEN = 2 * PAIRS
    FIRST = P * PAIRS
    REST = TOK - FIRST
    EPS = 1e-5
    FAR = -1.0e30
    RING = 4
    LANES = 3
    PARTS = 4
    assert 2 * D == 128 and F == 128 and FIRST <= 512 and HALF <= 512 and EVEN * D <= 512
    assert Q % RING == 0 and (STEPS - 4) % 2 == 0

    gates_dram = nc.dram_tensor("gates_dram", (STEPS, E, EVEN * P), f32)
    h2_dram = nc.dram_tensor("h2_dram", (STEPS, P, TILES, D), f32)

    ctx = ExitStack()
    with ctx:
        def sb(name, shape, dt=f32):
            return ctx.enter_context(nc.sbuf_tensor(name, shape, dt))

        def ps(name, banks):
            return ctx.enter_context(nc.psum_tensor(name, [128, 512 * banks], f32))

        def sem(name):
            return ctx.enter_context(nc.semaphore(name))

        tokw = sb("tokw", [K_IN + 1, D])
        cell = sb("cell", [2 * D, 2, D])
        rbias = sb("rbias", [2 * D, 2])
        rb = sb("rb", [2 * D, 1])
        w1f = sb("w1f", [2 * D, E, F])
        w1hi = sb("w1hi", [2 * D, E, F], f32r)
        w1lo = sb("w1lo", [2 * D, E, F], f32r)
        gwf = sb("gwf", [2 * D, E])
        gwhl = sb("gwhl", [2 * D, 2 * E], f32r)
        b1c = sb("b1c", [F, E])
        w2s = sb("w2s", [F, E, D])
        b2c = sb("b2c", [2 * D, Q])
        gbias = sb("gbias", [P, E])
        gam = sb("gam", [P, D])
        bet = sb("bet", [P, D])
        ident = sb("ident", [128, 128])
        rank_i = sb("rank_i", [P, E], i32)
        rank = sb("rank", [P, E])
        nhalf = sb("nhalf", [P, TILES])

        total = sb("total", [P, LANES, TILES])
        cen = sb("cen", [P, LANES, TILES, D])
        sq = sb("sq", [P, LANES, TILES, D])
        sumsq = sb("sumsq", [P, LANES, TILES])
        var = sb("var", [P, LANES, TILES])
        inv_std = sb("inv_std", [P, LANES, TILES])
        xcur = sb("xcur", [K_IN + 1, TOK])
        h1 = [sb(f"h1_{i}", [P, TILES, D]) for i in range(2)]
        xn1 = sb("xn1", [P, TILES, D])
        state = sb("state", [2 * D, 2, FIRST])
        h2 = sb("h2", [P, TILES, D])
        x2 = sb("x2", [P, TILES, D])
        x2hl = sb("x2hl", [P, TILES, 2, D], f32r)
        xt = [sb(f"xt{i}", [2 * D, TOK], f32r) for i in range(2)]
        lg = sb("lg", [P, TILES, E])
        hit = sb("hit", [P, TILES, E])
        best = [sb(f"best{i}", [P, TILES, E]) for i in range(2)]
        tv = sb("tv", [P, 9, TILES])
        gates = sb("gates", [P, EVEN, E])
        gt = sb("gt", [2 * E, FIRST])
        spread = [sb(f"spread{i}", [2 * D, Q, TOK]) for i in range(2)]
        hexp = [sb(f"hexp{i}", [F, TOK]) for i in range(RING)]
        prod = [sb(f"prod{i}", [2 * D, TOK]) for i in range(RING)]
        acc = [sb(f"acc{i}", [2 * D, TOK]) for i in range(2)]
        y = sb("y", [P, TILES, D])
        h2c = sb("h2c", [P, TILES, D])
        h2b = sb("h2b", [P, TILES, D])
        yn = sb("yn", [P, TILES, D])
        yo = sb("yo", [P, TILES, D])

        pZ = [ps(f"pZ{i}", 2) for i in range(2)]
        pO = ps("pO", 2)
        pA = ps("pA", 1)
        pB = ps("pB", 1)

        class Chain:

            def __init__(self, name, stages):
                self.sem, self.stages = sem(name), stages.split()

            def wait(self, eng, step, stage):
                eng.wait_ge(self.sem, step * len(self.stages) + self.stages.index(stage) + 1)

        EMBED = Chain("embed_stage", "h1 sum center rstd norm turned xn1t_odd xn1t")
        MIX = Chain("mix_stage", "pre hid_odd hid hid_turned h2_even h2 sum center rstd x2 hi lo "
                                 "turned_a turned_b xt_a xt_b")
        GATE = Chain("gate_stage", "logits hi_part biased max1 hit1 ranked1 first1 best1 without "
                                   "max2 hit2 ranked2 first2 best2 diff exp den p1 p2 g1 g2 gates turned gt")
        CLOSE = Chain("close_stage", "turned y_even y sum center gamma rstd norm out")
        NORM = Chain("norm_stage", "square sumsq var")
        FILL = 3

        def after(t, fill, steady):
            return fill if known(t, 0) else steady

        embed_loaded = sem("embed_weights_loaded")
        cell_loaded = sem("cell_and_gate_weights_loaded")
        experts_loaded = sem("expert_weights_loaded")
        xload = sem("x_loaded")
        consts = sem("constants_set")
        rb_set = sem("rb_set")
        rank_set = sem("rank_set")
        gw_split = sem("gate_w_split")
        w1_split = sem("w1_split")
        h1_kept = sem("h1_kept")
        h2_stored = sem("h2_stored")
        h2_loaded = sem("h2_loaded")
        h2b_set = sem("h2b_set")
        gt_stored = sem("gates_stored")
        spread_in = [sem(f"spread_loaded_{i}") for i in range(PARTS)]
        z_ready = sem("z_ready")
        h_ready = sem("h_ready")
        y_ready = sem("y_ready")
        p_ready = sem("product_ready")
        summed = sem("product_summed")
        stored = sem("out_stored")

        def halves(tensor):
            return tensor[:, :].rearrange("p (b c) -> p b c", b=2)[:, :, 0:HALF]

        def tiles_of(bank):
            return bank[0:P, 0:TILES * D].rearrange("p (i d) -> p i d", d=D)

        def lanes_of(embed=False, mix=False, close=False):
            return slice(0 if embed else 1 if mix else 2, 3 if close else 2 if mix else 1)

        def over_d(ap):
            return ap.unsqueeze(2).to_broadcast([P, TILES, D])

        def over_e(ap):
            return ap.unsqueeze(2).to_broadcast([P, TILES, E])

        def over_tiles(ap, n):
            return ap.unsqueeze(1).to_broadcast([P, TILES, n])

        def known(value, bound):
            return isinstance(value, int) and value < bound

        def run(eng, body):
            body(-2, 0, mix=True, embed=True)
            body(-1, 1, gate=True, mix=True, embed=True)
            body(0, 0, experts=True, gate=True, mix=True, embed=True)
            with eng.Fori(0, (STEPS - 4) // 2) as i:
                t = 2 * i + 1
                body(t, 1, experts=True, gate=True, mix=True, embed=True, close=True)
                body(t + 1, 0, experts=True, gate=True, mix=True, embed=True, close=True)
            body(STEPS - 3, 1, experts=True, gate=True, mix=True, close=True)
            body(STEPS - 2, 0, experts=True, gate=True, close=True)
            body(STEPS - 1, 1, experts=True, close=True)

        block = ctx.enter_context(nc.Block())

        embed_loads = [(tokw[0:K_IN, :], tok_w), (tokw[K_IN:K_IN + 1, :], tok_b.unsqueeze(0))]
        cell_loads, expert_loads = [], []
        for k in range(2):
            rows = slice(k * D, (k + 1) * D)
            cell_loads += [(cell[rows, k, :], w_ih), (cell[rows, 1 - k, :], w_hh),
                           (rbias[rows, 0:1], b_ih.unsqueeze(1)), (rbias[rows, 1:2], b_hh.unsqueeze(1)),
                           (gwf[rows, :], gate_w)]
            expert_loads += [(w1f[rows, :, :], w1)]
        cell_loads += [(gbias[:, :], gate_b.partition_broadcast(P))]
        expert_loads += [(b1c[:, :], b1), (w2s[:, :, :], w2), (b2c[:, :], b2),
                         (gam[:, :], gamma.partition_broadcast(P)), (bet[:, :], beta.partition_broadcast(P))]
        CELL_LOADED = 16 * len(cell_loads)
        EXPERTS_LOADED = 16 * len(expert_loads)
        fills = [(xcur[K_IN:K_IN + 1, :], 1.0), (ident[:, :], 0.0), (nhalf[:, :], -0.5), (state[:, :, :], 0.0),
                 (gates[:, :, :], 0.0)]
        ONES_SET, STATE_SET, RANK_SET, IDENT_SET = 1, 4, len(fills) + 1, len(fills) + 2

        @block.sync
        def _(sp):
            def load_x(s):
                if not known(s, 1):
                    EMBED.wait(sp, s - 1, "h1")
                sp.dma_start(xcur[0:K_IN, :], x_in[:, bass.ds(s * TOK, TOK)]).then_inc(xload, 16)

            def keep_h2(s):
                MIX.wait(sp, s, "h2")
                sp.dma_start(h2_dram[bass.ds(s, 1), :, :, :].rearrange("s p i d -> (s p) i d"),
                             h2[:, :, :]).then_inc(h2_stored, 16)

            def fetch_h2(s):
                sp.wait_ge(h2_stored, 16 * s + 16)
                sp.dma_start(h2c[:, :, :], h2_dram[bass.ds(s, 1), :, :, :].rearrange("s p i d -> (s p) i d"))\
                    .then_inc(h2_loaded, 16)

            def spread_gates(s, par):
                GATE.wait(sp, s, "gt")
                rows = gates_dram[bass.ds(s, 1), :, :].rearrange("s e (i c) -> (s e) i c", i=PAIRS)
                for k in range(2):
                    n = TILES // 2 + 1 - k
                    sp.dma_start(rows[:, 0:n, k * P:(k + 1) * P],
                                 gt[k * E:(k + 1) * E, 0:n * P].rearrange("e (i p) -> e i p", p=P))\
                        .then_inc(gt_stored, 16)
                sp.wait_ge(gt_stored, 32 * s + 32)
                if not known(s, 2):
                    sp.wait_ge(p_ready, (s - 1) * 2 * Q)
                for part in range(PARTS):
                    for k in range(2):
                        q0, n = part * (Q // PARTS), Q // PARTS
                        src = gates_dram[bass.ds(s, 1), :, 0:TOK].rearrange("s (q k) n -> k s q n", k=2)[k]
                        sp.dma_start(spread[par][k * D:(k + 1) * D, q0:q0 + n, :],
                                     src[:, q0:q0 + n, :].to_broadcast([D, n, TOK])).then_inc(spread_in[part], 16)

            def store(s):
                CLOSE.wait(sp, s, "out")
                sp.dma_start(out[bass.ds(s, 1), :, :, :].rearrange("s p i d -> (s p) i d"), yo[:, :, :])\
                    .then_inc(stored, 16)

            def body(t, par, experts=False, gate=False, mix=False, embed=False, close=False):
                if embed and (known(t, 0) or not known(t, 1)):
                    load_x(t + 3)
                if known(t, -1):
                    for dst, src in expert_loads:
                        sp.dma_start(dst, src).then_inc(experts_loaded, 16)
                if close:
                    fetch_h2(t - 1)
                if mix:
                    keep_h2(t + 2)
                if known(t, 0) and gate:
                    load_x(t + 4)
                if gate:
                    spread_gates(t + 1, 1 - par)
                if close:
                    store(t - 1)

            load_x(0)
            for dst, src in embed_loads:
                sp.dma_start(dst, src).then_inc(embed_loaded, 16)
            for dst, src in cell_loads:
                sp.dma_start(dst, src).then_inc(cell_loaded, 16)
            run(sp, body)
            fetch_h2(STEPS - 1)
            store(STEPS - 1)
            sp.wait_ge(stored, 16 * STEPS + 16)

        @block.gpsimd
        def _(pool):
            for k, (dst, value) in enumerate(fills):
                if k:
                    pool.wait_ge(consts, k)
                nc.gpsimd.memset(dst, value).then_inc(consts, 1)
            pool.wait_ge(consts, len(fills))
            nc.gpsimd.iota(rank_i[:, :], pattern=[[-1, E]], base=E, channel_multiplier=0).then_inc(consts, 1)
            pool.wait_ge(consts, RANK_SET)
            nc.gpsimd.affine_select(out=ident[:, :], in_=ident[:, :], compare_op=ALU.not_equal, fill=1.0,
                                    base=0, pattern=[[-1, 128]], channel_multiplier=1).then_inc(consts, 1)
            pool.wait_ge(consts, IDENT_SET)
            nc.gpsimd.memset(yo[:, :, :], 0.0).then_inc(stored, 16)

            def rstd(chain, n, lane):
                NORM.wait(pool, n, "var")
                nc.gpsimd.tensor_tensor(inv_std[:, lane, :], var[:, lane, :], nhalf[:, :], ALU.pow)\
                    .then_inc(chain.sem, 1)

            def add(step, q, par):
                n = step * Q + q
                pool.wait_ge(p_ready, 2 * n + 2)
                if q == 0:
                    MIX.wait(pool, step, "xt_b")
                    sofar = xt[par][:, :].bitcast(f32)
                else:
                    pool.wait_ge(summed, n)
                    sofar = acc[par][:, :]
                nc.gpsimd.tensor_tensor(acc[par][:, :], sofar, prod[q % RING][:, :], ALU.add).then_inc(summed, 1)

            def add_beta(s):
                pool.wait_ge(experts_loaded, EXPERTS_LOADED)
                pool.wait_ge(h2_loaded, 16 * s + 16)
                nc.gpsimd.tensor_tensor(h2b[:, :, :], h2c[:, :, :], over_tiles(bet[:, :], D), ALU.add)\
                    .then_inc(h2b_set, 1)

            def body(t, par, experts=False, gate=False, mix=False, embed=False, close=False):
                for u in range(E):
                    if experts and u % 2 == 1:
                        if u > 1:
                            add(t, u // 2 - 1, par)
                        elif not known(t, 1):
                            add(t - 1, Q - 1, 1 - par)
                    if close and u == 2:
                        add_beta(t - 1)
                    if known(t, 0) and gate and u == 5:
                        pool.wait_ge(w1_split, 1)
                        nc.gpsimd.tensor_tensor(w1lo[:, :, :], w1f[:, :, :], w1hi[:, :, :].bitcast(f32), ALU.subtract)\
                            .then_inc(w1_split, 1)
                    if mix and u == 11:
                        rstd(MIX, t + FILL, 1)
                    if close and u == 12:
                        rstd(CLOSE, t + FILL, 2)
                    if embed and u == 12:
                        rstd(EMBED, t + FILL, 0)

            rstd(EMBED, 0, 0)
            run(pool, body)
            add(STEPS - 1, Q - 1, (STEPS - 1) % 2)
            add_beta(STEPS - 1)
            rstd(CLOSE, STEPS + FILL, 2)

        @block.scalar
        def _(act):
            def keep_h1(s, par):
                EMBED.wait(act, s, "h1")
                if not known(s, 2):
                    MIX.wait(act, s - 2, "h2")
                nc.scalar.activation(h1[par][:, :, :], tiles_of(pB), ACT.Copy).then_inc(h1_kept, 1)

            def keep_xt(s, par):
                MIX.wait(act, s, "turned_b")
                if not known(s, 2):
                    act.wait_ge(summed, (s - 2) * Q + 1)
                nc.scalar.activation(xt[par][:, 0:FIRST], pA[:, 0:FIRST], ACT.Copy).then_inc(MIX.sem, 1)
                nc.scalar.activation(xt[par][:, FIRST:TOK], pB[:, 0:REST], ACT.Copy).then_inc(MIX.sem, 1)

            def square(lanes):
                nc.scalar.activation(sq[:, lanes, :, :], cen[:, lanes, :, :], ACT.Square).then_inc(NORM.sem, 1)

            def keep_xn1t(s):
                EMBED.wait(act, s, "turned")
                if not known(s, 1):
                    MIX.wait(act, s - 1, "pre")
                if known(s, 1):
                    act.wait_ge(consts, STATE_SET)
                nc.scalar.activation(state[D:2 * D, 1, 0:REST], pA[D:2 * D, 0:REST], ACT.Copy).then_inc(EMBED.sem, 1)
                nc.scalar.activation(state[0:D, 0, :], pA[0:D, 0:FIRST], ACT.Copy).then_inc(EMBED.sem, 1)

            def new_hidden(s):
                MIX.wait(act, s, "pre")
                nc.scalar.activation(state[0:D, 1, 0:REST], pA[0:D, 0:REST], ACT.Tanh, bias=rb[0:D, 0:1])\
                    .then_inc(MIX.sem, 1)
                nc.scalar.activation(state[D:2 * D, 0, :], pA[D:2 * D, 0:FIRST], ACT.Tanh, bias=rb[D:2 * D, 0:1])\
                    .then_inc(MIX.sem, 1)

            def body(t, par, experts=False, gate=False, mix=False, embed=False, close=False):
                for u in range(E):
                    if experts:
                        n = t * E + u
                        act.wait_ge(z_ready, n + 1)
                        if not known(n, RING):
                            act.wait_ge(y_ready, t * E + 2 * (u // 2) - RING + 2)
                        nc.scalar.activation(hexp[u % RING][:, :].rearrange("p (b c) -> p b c", b=2),
                                             halves(pZ[u % 2]), ACT.Relu, bias=b1c[:, u:u + 1])\
                            .then_inc(h_ready, 1)
                    if gate and u == 1:
                        keep_xt(t + 1, 1 - par)
                    if embed and u == (3 if known(t, -1) else 5):
                        keep_h1(t + 3, 1 - par)
                    if mix and u == 2:
                        keep_xn1t(t + 2)
                    if mix and u == 3:
                        new_hidden(t + 2)
                    if known(t, 0) and gate and u == 4:
                        act.wait_ge(experts_loaded, EXPERTS_LOADED)
                        nc.scalar.activation(w1hi[:, :, :], w1f[:, :, :], ACT.Copy).then_inc(w1_split, 1)
                    if gate and u == 6:
                        GATE.wait(act, t + 1, "diff")
                        nc.scalar.activation(tv[:, 5, :], tv[:, 4, :], ACT.Exp).then_inc(GATE.sem, 1)
                    if gate and u == 10:
                        GATE.wait(act, t + 1, "turned")
                        if not known(t, 0):
                            act.wait_ge(gt_stored, 32 * t + 32)
                        nc.scalar.activation(gt[:, :], pB[0:2 * E, 0:FIRST], ACT.Copy).then_inc(GATE.sem, 1)
                    if u == after(t, 6, 11) and (mix or close):
                        if embed:
                            EMBED.wait(act, t + 3, "center")
                        if mix:
                            MIX.wait(act, t + 2, "center")
                        if close:
                            CLOSE.wait(act, t - 1, "center")
                        square(lanes_of(embed, mix, close))
                    if mix and u == 15:
                        MIX.wait(act, t + 2, "x2")
                        nc.scalar.activation(x2hl[:, :, 0, :], x2[:, :, :], ACT.Copy).then_inc(MIX.sem, 1)

            keep_h1(0, 0)
            EMBED.wait(act, 0, "center")
            square(lanes_of(embed=True))
            act.wait_ge(cell_loaded, CELL_LOADED)
            nc.scalar.activation(gwhl[:, 0:E], gwf[:, :], ACT.Copy).then_inc(gw_split, 1)
            act.wait_ge(rb_set, 1)
            run(act, body)
            CLOSE.wait(act, STEPS - 1, "center")
            square(lanes_of(close=True))

        @block.vector
        def _(dve):
            def norm_sum(chain, s, lane, src):
                nc.vector.tensor_reduce(total[:, lane, :], src, X, ALU.add).then_inc(chain.sem, 1)

            def norm_center(chain, s, lane, src):
                chain.wait(dve, s, "sum")
                nc.vector.scalar_tensor_tensor(out=cen[:, lane, :, :], in0=over_d(total[:, lane, :]), scalar=-1.0 / D,
                                               in1=src, op0=ALU.mult, op1=ALU.add).then_inc(chain.sem, 1)

            def norm_var(n, lanes):
                NORM.wait(dve, n, "square")
                nc.vector.tensor_reduce(sumsq[:, lanes, :], sq[:, lanes, :, :], X, ALU.add).then_inc(NORM.sem, 1)
                NORM.wait(dve, n, "sumsq")
                nc.vector.tensor_scalar(var[:, lanes, :], sumsq[:, lanes, :], 1.0 / D, EPS, ALU.mult, ALU.add)\
                    .then_inc(NORM.sem, 1)

            def norm_scale(chain, s, lane, dst):
                chain.wait(dve, s, "rstd")
                nc.vector.tensor_tensor(dst, cen[:, lane, :, :], over_d(inv_std[:, lane, :]), ALU.mult)\
                    .then_inc(chain.sem, 1)

            def embed_sum(s, par):
                dve.wait_ge(h1_kept, s + 1)
                norm_sum(EMBED, s, 0, h1[par][:, :, :])

            def close_add(s):
                CLOSE.wait(dve, s, "turned")
                for bank, first, end in ((pA, 0, PAIRS), (pB, PAIRS, TILES)):
                    parts = bank[0:P, 0:(end - first) * 2 * D].rearrange("p (i k d) -> p i d k", k=2, d=D)
                    nc.vector.tensor_reduce(y[:, first:end, :], parts, X, ALU.add).then_inc(CLOSE.sem, 1)

            def close_sum(s):
                CLOSE.wait(dve, s, "y")
                norm_sum(CLOSE, s, 2, y[:, :, :])

            def bias_logits(s):
                GATE.wait(dve, s, "logits")
                parts = pB[0:P, 0:TILES * 2 * E].rearrange("p (i k e) -> p k i e", e=E, k=2)
                nc.vector.tensor_tensor(lg[:, :, :], parts[:, 0, :, :], over_tiles(gbias[:, :], E), ALU.add)\
                    .then_inc(GATE.sem, 1)
                GATE.wait(dve, s, "hi_part")
                nc.vector.tensor_tensor(lg[:, :, :], parts[:, 1, :, :], lg[:, :, :], ALU.add).then_inc(GATE.sem, 1)

            def find(s, k):
                top, mark, one = tv[:, k, :], tv[:, 2 + k, :], best[k]
                GATE.wait(dve, s, "without" if k else "biased")
                nc.vector.tensor_reduce(top, lg[:, :, :], X, ALU.max).then_inc(GATE.sem, 1)
                GATE.wait(dve, s, f"max{k + 1}")
                nc.vector.tensor_tensor(hit[:, :, :], lg[:, :, :], over_e(top), ALU.is_equal).then_inc(GATE.sem, 1)
                GATE.wait(dve, s, f"hit{k + 1}")
                nc.vector.tensor_tensor(hit[:, :, :], hit[:, :, :], over_tiles(rank[:, :], E), ALU.mult)\
                    .then_inc(GATE.sem, 1)
                GATE.wait(dve, s, f"ranked{k + 1}")
                nc.vector.tensor_reduce(mark, hit[:, :, :], X, ALU.max).then_inc(GATE.sem, 1)
                GATE.wait(dve, s, f"first{k + 1}")
                nc.vector.tensor_tensor(one[:, :, :], hit[:, :, :], over_e(mark), ALU.is_equal).then_inc(GATE.sem, 1)

            def find_first(s):
                find(s, 0)
                GATE.wait(dve, s, "best1")
                nc.vector.scalar_tensor_tensor(out=lg[:, :, :], in0=best[0][:, :, :], scalar=FAR, in1=lg[:, :, :],
                                               op0=ALU.mult, op1=ALU.add).then_inc(GATE.sem, 1)

            def find_second(s):
                find(s, 1)
                nc.vector.tensor_tensor(tv[:, 4, :], tv[:, 1, :], tv[:, 0, :], ALU.subtract).then_inc(GATE.sem, 1)

            def gate_weights(s):
                GATE.wait(dve, s, "exp")
                nc.vector.tensor_scalar(tv[:, 6, :], tv[:, 5, :], 1.0, None, ALU.add).then_inc(GATE.sem, 1)
                GATE.wait(dve, s, "den")
                nc.vector.reciprocal(tv[:, 7, :], tv[:, 6, :]).then_inc(GATE.sem, 1)
                GATE.wait(dve, s, "p1")
                nc.vector.tensor_tensor(tv[:, 8, :], tv[:, 5, :], tv[:, 7, :], ALU.mult).then_inc(GATE.sem, 1)
                GATE.wait(dve, s, "p2")
                nc.vector.tensor_tensor(best[0][:, :, :], best[0][:, :, :], over_e(tv[:, 7, :]), ALU.mult)\
                    .then_inc(GATE.sem, 1)
                nc.vector.tensor_tensor(best[1][:, :, :], best[1][:, :, :], over_e(tv[:, 8, :]), ALU.mult)\
                    .then_inc(GATE.sem, 1)
                GATE.wait(dve, s, "g2")
                nc.vector.tensor_tensor(gates[:, 0:TILES, :], best[0][:, :, :], best[1][:, :, :], ALU.add)\
                    .then_inc(GATE.sem, 1)

            def product(step, q, par):
                n = step * Q + q
                if q % (Q // PARTS) == 0:
                    dve.wait_ge(spread_in[q // (Q // PARTS)], (step + 1) * 2 * 16)
                if not known(n, RING):
                    dve.wait_ge(summed, n - RING + 1)
                for b in range(2):
                    dve.wait_ge(y_ready, 2 * n + b + 1)
                    nc.vector.scalar_tensor_tensor(
                        out=prod[q % RING][:, b * HALF:(b + 1) * HALF], in0=halves(pO)[:, b, :],
                        scalar=b2c[:, q:q + 1], in1=spread[par][:, q, b * HALF:(b + 1) * HALF],
                        op0=ALU.add, op1=ALU.mult).then_inc(p_ready, 1)

            def close_gamma(s):
                CLOSE.wait(dve, s, "center")
                nc.vector.tensor_tensor(yn[:, :, :], cen[:, 2, :, :], over_tiles(gam[:, :], D), ALU.mult)\
                    .then_inc(CLOSE.sem, 1)

            def close_out(s):
                CLOSE.wait(dve, s, "rstd")
                nc.vector.tensor_tensor(yn[:, :, :], yn[:, :, :], over_d(inv_std[:, 2, :]), ALU.mult)\
                    .then_inc(CLOSE.sem, 1)
                CLOSE.wait(dve, s, "norm")
                dve.wait_ge(h2b_set, s + 1)
                dve.wait_ge(stored, 16 * s + 16)
                nc.vector.tensor_tensor(yo[:, :, :], yn[:, :, :], h2b[:, :, :], ALU.add).then_inc(CLOSE.sem, 1)

            def body(t, par, experts=False, gate=False, mix=False, embed=False, close=False):
                g, s, a, c = t + 1, t + 2, t + 3, t - 1
                for u in range(E):
                    if experts and u % 2 == 1:
                        if u > 1:
                            product(t, u // 2 - 1, par)
                        elif not known(t, 1):
                            product(t - 1, Q - 1, 1 - par)
                    if mix and u == 0:
                        norm_scale(EMBED, s, 0, xn1[:, :, :])
                    if known(t, -1) and u == 4:
                        embed_sum(a, 1 - par)
                        norm_center(EMBED, a, 0, h1[1 - par][:, :, :])
                    if gate and u == 3:
                        bias_logits(g)
                        find_first(g)
                    if mix and u == 5:
                        MIX.wait(dve, s, "hid_turned")
                        dve.wait_ge(h1_kept, s + 1)
                        if not known(s, 1):
                            dve.wait_ge(h2_stored, 16 * s)
                        for odd, n in ((0, PAIRS), (1, TILES // 2)):
                            column = 0 if odd else (TILES // 2 + 1) * D
                            hidden = pA[0:P, column:column + n * D].rearrange("p (i d) -> p i d", d=D)
                            nc.vector.tensor_tensor(h2[:, odd::2, :], hidden, h1[par][:, odd::2, :], ALU.add)\
                                .then_inc(MIX.sem, 1)
                    if gate and u == 5:
                        find_second(g)
                    if gate and u == 7:
                        gate_weights(g)
                    if close and u == 7:
                        close_add(c)
                    if mix and u == 5:
                        MIX.wait(dve, s, "h2")
                        norm_sum(MIX, s, 1, h2[:, :, :])
                    if embed and not known(t, -1) and u == after(t, 5, 7):
                        embed_sum(a, 1 - par)
                    if close and u == 9:
                        close_sum(c)
                    if mix and u == after(t, 5, 9):
                        norm_center(MIX, s, 1, h2[:, :, :])
                    if embed and not known(t, -1) and u == after(t, 5, 9):
                        norm_center(EMBED, a, 0, h1[1 - par][:, :, :])
                    if close and u == 9:
                        norm_center(CLOSE, c, 2, y[:, :, :])
                    if close and u == 11:
                        close_gamma(c)
                    if u == after(t, 8, 11) and (mix or close):
                        norm_var(t + FILL, lanes_of(embed, mix, close))
                    if mix and u == 13:
                        norm_scale(MIX, s, 1, x2[:, :, :])
                    if mix and u == 15:
                        MIX.wait(dve, s, "hi")
                        nc.vector.tensor_tensor(x2hl[:, :, 1, :], x2[:, :, :], x2hl[:, :, 0, :].bitcast(f32),
                                                ALU.subtract).then_inc(MIX.sem, 1)
                    if close and u == 15:
                        close_out(c)

            embed_sum(0, 0)
            norm_center(EMBED, 0, 0, h1[0][:, :, :])
            norm_var(0, lanes_of(embed=True))
            dve.wait_ge(cell_loaded, CELL_LOADED)
            nc.vector.tensor_tensor(rb[:, :], rbias[:, 0:1], rbias[:, 1:2], ALU.add).then_inc(rb_set, 1)
            dve.wait_ge(gw_split, 1)
            nc.vector.tensor_tensor(gwhl[:, E:2 * E], gwf[:, :], gwhl[:, 0:E].bitcast(f32), ALU.subtract)\
                .then_inc(gw_split, 1)
            dve.wait_ge(consts, RANK_SET)
            nc.vector.tensor_copy(rank[:, :], rank_i[:, :]).then_inc(rank_set, 1)
            dve.wait_ge(rank_set, 1)
            run(dve, body)
            last = STEPS - 1
            product(last, Q - 1, last % 2)
            close_add(last)
            close_sum(last)
            norm_center(CLOSE, last, 2, y[:, :, :])
            close_gamma(last)
            norm_var(STEPS + FILL, lanes_of(close=True))
            close_out(last)

        @block.tensor
        def _(pe):
            pe.wait_ge(embed_loaded, 16 * len(embed_loads))
            pe.wait_ge(consts, ONES_SET)

            def embed_in(s):
                pe.wait_ge(xload, 16 * s + 16)
                if not known(s, 2):
                    GATE.wait(pe, s - 2, "biased")
                elif not known(s, 1):
                    EMBED.wait(pe, s - 1, "xn1t")
                for i in range(TILES):
                    last = nc.tensor.matmul(tiles_of(pB)[:, i, :], xcur[:, i * P:(i + 1) * P], tokw[:, :],
                                            start=True, stop=True)
                last.then_inc(EMBED.sem, 1)

            def embed_turn(s):
                EMBED.wait(pe, s, "norm")
                if not known(s, 1):
                    MIX.wait(pe, s - 1, "xt_b")
                for i in range(PAIRS):
                    n = min(2, TILES - 2 * i)
                    last = nc.tensor.transpose(pA[0:n * D, i * P:(i + 1) * P],
                                               xn1[:, 2 * i:2 * i + n, :].rearrange("p a d -> p (a d)"),
                                               ident[0:P, 0:P])
                last.then_inc(EMBED.sem, 1)

            def recur(s):
                EMBED.wait(pe, s, "xn1t")
                nc.tensor.matmul(pA[D:2 * D, 0:FIRST], cell[:, 0, :], state[:, 0, :], start=True, stop=True)
                nc.tensor.matmul(pA[0:D, 0:REST], cell[:, 1, :], state[:, 1, 0:REST], start=True, stop=True)\
                    .then_inc(MIX.sem, 1)

            def hidden_turn(s):
                MIX.wait(pe, s, "hid")
                for i in [*range(1, TILES, 2), *reversed(range(0, TILES, 2))]:
                    column = (i // 2 if i % 2 else TILES // 2 + i // 2) * D
                    last = nc.tensor.transpose(pA[0:P, column:column + 2 * D],
                                               state[:, 1 if i % 2 else 0, (i // 2) * P:(i // 2 + 1) * P], ident[:, :])
                last.then_inc(MIX.sem, 1)

            def x2_turn(s):
                MIX.wait(pe, s, "lo")
                if not known(s, 1):
                    GATE.wait(pe, s - 1, "gt")
                for bank, first, end in ((pA, 0, PAIRS), (pB, PAIRS, TILES)):
                    for i in range(first, end):
                        last = nc.tensor.transpose(bank[:, (i - first) * P:(i - first + 1) * P],
                                                   x2hl[:, i, :, :].bitcast(f32).rearrange("p a d -> p (a d)"),
                                                   ident[0:P, 0:P])
                    last.then_inc(MIX.sem, 1)

            def logits(s, par):
                MIX.wait(pe, s, "xt_b")
                if known(s, 1):
                    pe.wait_ge(gw_split, 2)
                for i in range(TILES):
                    last = nc.tensor.matmul(pB[0:P, i * 2 * E:(i + 1) * 2 * E], xt[par][:, i * P:(i + 1) * P],
                                            gwhl[:, :], start=True, stop=True)
                last.then_inc(GATE.sem, 1)

            def gates_turn(s, embed, close):
                GATE.wait(pe, s, "gates")
                if close:
                    CLOSE.wait(pe, s - 2, "y")
                elif embed:
                    pe.wait_ge(h1_kept, s + 3)
                for i in range(PAIRS):
                    last = nc.tensor.transpose(pB[0:2 * E, i * P:(i + 1) * P],
                                               gates[:, 2 * i:2 * i + 2, :].rearrange("p a e -> p (a e)"),
                                               ident[0:P, 0:P])
                last.then_inc(GATE.sem, 1)

            def first_layer(t, e, par):
                n = t * E + e
                if e == 0:
                    MIX.wait(pe, t, "xt_b")
                if known(n, 1):
                    pe.wait_ge(w1_split, 2)
                if not known(n, 2):
                    pe.wait_ge(h_ready, n - 1)
                for b in range(2):
                    for k, w in enumerate((w1hi, w1lo)):
                        last = nc.tensor.matmul(halves(pZ[e % 2])[:, b, :], w[:, e, :],
                                                xt[par][:, b * HALF:(b + 1) * HALF], start=(k == 0), stop=(k == 1))
                last.then_inc(z_ready, 1)

            def second_layer(t, q):
                n = t * Q + q
                pe.wait_ge(h_ready, 2 * n + 2)
                for b in range(2):
                    if not known(n, 1):
                        pe.wait_ge(p_ready, 2 * n - 1 + b)
                    for k in range(2):
                        e = 2 * q + k
                        last = nc.tensor.matmul(halves(pO)[k * D:(k + 1) * D, b, :], w2s[:, e, :],
                                                hexp[e % RING][:, b * HALF:(b + 1) * HALF], start=True, stop=True)
                    last.then_inc(y_ready, 1)

            def sum_turn(s, par, gate=False, mix=False, embed=False):
                pe.wait_ge(summed, s * Q + Q)
                if mix:
                    MIX.wait(pe, s + 3, "h2")
                if embed:
                    pe.wait_ge(h1_kept, s + 5)
                elif gate:
                    GATE.wait(pe, s + 2, "biased")
                for bank, first, end in ((pA, 0, PAIRS), (pB, PAIRS, TILES)):
                    for i in range(first, end):
                        last = nc.tensor.transpose(bank[0:P, (i - first) * 2 * D:(i - first + 1) * 2 * D],
                                                   acc[par][:, i * P:(i + 1) * P], ident[:, :])
                last.then_inc(CLOSE.sem, 1)

            def body(t, par, experts=False, gate=False, mix=False, embed=False, close=False):
                for u in range(E):
                    if experts:
                        first_layer(t, u, par)
                    if gate and u == 3:
                        logits(t + 1, 1 - par)
                    if mix and u == 3:
                        recur(t + 2)
                    if gate and u == 10:
                        gates_turn(t + 1, embed, close)
                    if experts and u % 2 == 1:
                        if u > 1:
                            second_layer(t, u // 2 - 1)
                        elif not known(t, 1):
                            second_layer(t - 1, Q - 1)
                    if mix and u == after(t, 4, 5):
                        hidden_turn(t + 2)
                    if embed and u == (3 if known(t, -1) else 5):
                        embed_in(t + 3)
                    if close and u == 7:
                        sum_turn(t - 1, 1 - par, gate, mix, embed)
                    if gate and u == 1:
                        x2_turn(t + 1)
                    if mix and u == 2:
                        embed_turn(t + 2)

            embed_in(0)
            pe.wait_ge(consts, IDENT_SET)
            pe.wait_ge(cell_loaded, CELL_LOADED)
            run(pe, body)
            second_layer(STEPS - 1, Q - 1)
            sum_turn(STEPS - 1, (STEPS - 1) % 2)


def kernel(**inputs):
    import numpy as np
    import concourse.bacc as bacc
    from concourse import mybir as mb
    from concourse.bass_utils import run_bass_kernel_spmd

    steps, _, height, width = inputs["x"].shape
    patch = 8
    rows, cols = height // patch, width // patch
    d = inputs["L0_tok_W"].shape[0]
    tiles = 7
    p = rows * cols // tiles

    def a(name):
        return np.asarray(inputs["L0_" + name])

    x = np.asarray(inputs["x"]).reshape(steps, rows, patch, cols, patch).transpose(2, 4, 0, 1, 3)
    x = x.reshape(patch * patch, steps, p, tiles).transpose(0, 1, 3, 2).reshape(patch * patch, -1)
    arrays = {
        "x_in": x, "tok_w": a("tok_W").T, "tok_b": a("tok_b"), "w_ih": a("attn_W_ih").T, "w_hh": a("attn_W_hh").T,
        "b_ih": a("attn_b_ih"), "b_hh": a("attn_b_hh"), "gate_w": a("ffn_gate_w"), "gate_b": a("ffn_gate_b"),
        "w1": a("ffn_w1").transpose(1, 0, 2), "b1": a("ffn_b1").T, "w2": a("ffn_w2").transpose(1, 0, 2),
        "b2": a("ffn_b2").reshape(-1, 2, d).transpose(1, 2, 0).reshape(2 * d, -1), "gamma": a("ffn_gamma"), "beta": a("ffn_beta"),
    }
    arrays = {k: np.ascontiguousarray(v) for k, v in arrays.items()}
    nc = bacc.Bacc("TRN2", target_bir_lowering=False, num_devices=1)
    args = [nc.dram_tensor(k, v.shape, mb.dt.from_np(v.dtype), kind="ExternalInput").ap() for k, v in arrays.items()]
    out = nc.dram_tensor("out", (steps, p, tiles, d), mb.dt.float32, kind="ExternalOutput").ap()
    vit_tower_kernel(nc, *args, out)
    r = run_bass_kernel_spmd(nc, [arrays], core_ids=[0])
    return r.results[0]["out"].reshape(steps, rows * cols, d)
```
